# Optimizing a Trainium2 kernel written in Bass

```python
import numpy as np
import jax
import jax.numpy as jnp

def _softmax(x, axis=-1):
    return jax.nn.softmax(x, axis=axis)

def _gelu(x):
    return jax.nn.gelu(x, approximate=True)

def _silu(x):
    return jax.nn.silu(x)

def _sigmoid(x):
    return jax.nn.sigmoid(x)

def _layernorm(x, axis=-1, eps=1e-05):
    m = jnp.mean(x, axis=axis, keepdims=True)
    v = jnp.var(x, axis=axis, keepdims=True)
    return (x - m) / jnp.sqrt(v + eps)

def _scatter_add(tgt, idx, src, axis=0):
    return tgt.at[idx].add(src)

def _segment_sum(src, seg, n):
    return jax.ops.segment_sum(src, seg, n)
kernel_name = 'mk_cond_resid_d4_seqx_r8_edc30a'

def setup_inputs(seed: int=0):
    np.random.seed(seed)
    _w = jnp.asarray

    def _rec_inputs():
        import jax
        import jax.numpy as jnp
        _rk = jax.random.key(seed)
        x = -0.0003929 + 0.9999 * jax.random.normal(jax.random.fold_in(_rk, 1), (32, 32, 128), jnp.float32)
        _lenS = 32 - jax.random.randint(jax.random.fold_in(_rk, 7), (32,), 0, max(1, 32 // 4) + 1, jnp.int32)
        _lenS2 = 32 - jax.random.randint(jax.random.fold_in(_rk, 8), (32,), 0, max(1, 32 // 4) + 1, jnp.int32)
        itok_B_0_63 = jax.random.randint(jax.random.fold_in(_rk, 11), (32,), 0, 64, jnp.int32)
        itok_B_0_2 = jax.random.randint(jax.random.fold_in(_rk, 12), (32,), 0, 3, jnp.int32)
        itok_B_0_7 = jax.random.randint(jax.random.fold_in(_rk, 13), (32,), 0, 8, jnp.int32)
        return (x, itok_B_0_63, itok_B_0_2, itok_B_0_7)
    x, itok_B_0_63, itok_B_0_2, itok_B_0_7 = _rec_inputs()

    def _L0_cond_setup():
        import jax, jax.numpy as jnp
        import numpy as np
        NUM_CATEGORIES = 64
        INPUT_DIM = 128
        HIDDEN_DIM = 128
        B = 32
        S = 64
        key = jax.random.key(seed)
        kx, kc, kw = jax.random.split(key, 3)
        x = jax.random.normal(kx, (B, S, INPUT_DIM), dtype=jnp.float32)
        cat_ids = jax.random.randint(kc, (B,), 0, NUM_CATEGORIES, dtype=jnp.int32)
        W = 0.02 * jax.random.normal(kw, (NUM_CATEGORIES, INPUT_DIM, HIDDEN_DIM), dtype=jnp.float32)
        b = jnp.zeros((NUM_CATEGORIES, HIDDEN_DIM), dtype=jnp.float32)
        return {'x': x, 'cat_ids': cat_ids, 'W': W, 'b': b}
    _L0_cond_all = _L0_cond_setup()
    _L0_cond_in = {k: v for k, v in _L0_cond_all.items() if k in ('W', 'b')}
    del _L0_cond_all

    def _L1_cond_setup():
        import jax, jax.numpy as jnp
        import numpy as np
        NEG_INF = -1e+30
        key = jax.random.key(seed)
        k1, k2, k3, k4, k5 = jax.random.split(key, 5)
        B, S, D, A = (16, 128, 128, 32)
        hidden = jax.random.normal(k1, (B, S, D), dtype=jnp.float32)
        W1 = jax.random.normal(k2, (D, A), dtype=jnp.float32) / np.sqrt(D)
        b1 = jax.random.normal(k3, (A,), dtype=jnp.float32) * 0.01
        v = jax.random.normal(k4, (A,), dtype=jnp.float32) / np.sqrt(A)
        prompt_type_ids = jax.random.randint(k5, (B,), 0, 3, dtype=jnp.int32)
        return {'hidden': hidden, 'W1': W1, 'b1': b1, 'v': v, 'prompt_type_ids': prompt_type_ids}
    _L1_cond_all = _L1_cond_setup()
    _L1_cond_in = {k: v for k, v in _L1_cond_all.items() if k in ('W1', 'b1', 'v')}
    del _L1_cond_all

    def _L2_cond_setup():
        import jax, jax.numpy as jnp
        import numpy as np
        S, O, H = (8, 128, 128)
        B, N = (32, 64)
        key = jax.random.key(seed)
        k1, k2, k3, k4 = jax.random.split(key, 4)
        x = jax.random.normal(k1, (B, N, H), dtype=jnp.float32)
        subject_id = jax.random.randint(k2, (B,), 0, S)
        wbound = jnp.sqrt(2.0 / 6.0) * jnp.sqrt(3.0 / H)
        weight = jax.random.uniform(k3, (S, O, H), minval=-wbound, maxval=wbound, dtype=jnp.float32)
        bbound = 1.0 / jnp.sqrt(H)
        bias = jax.random.uniform(k4, (S, O), minval=-bbound, maxval=bbound, dtype=jnp.float32)
        return {'x': x, 'subject_id': subject_id, 'weight': weight, 'bias': bias}
    _L2_cond_all = _L2_cond_setup()
    _L2_cond_in = {k: v for k, v in _L2_cond_all.items() if k in ('weight', 'bias')}
    del _L2_cond_all

    def _L3_cond_setup():
        import jax, jax.numpy as jnp
        import numpy as np
        B, S, D, F = (32, 64, 128, 512)
        R_COMMON, R_DOMAIN, E = (16, 16, 8)
        ALPHA = 2.0

        def _expert_lora(x, expert_ids, Wa, Wb):
            Ab = Wa[expert_ids]
            Bb = Wb[expert_ids]
            low = jnp.einsum('bsd,brd->bsr', x, Ab)
            return ALPHA * jnp.einsum('bsr,bor->bso', low, Bb)
        key = jax.random.key(seed)
        ks = jax.random.split(key, 12)
        sd = lambda k, shape: jax.random.normal(k, shape, dtype=jnp.float32) * (1.0 / np.sqrt(shape[-1]))
        return {'hidden_states': jax.random.normal(ks[0], (B, S, D), dtype=jnp.float32), 'expert_ids': jax.random.randint(ks[1], (B,), 0, E, dtype=jnp.int32), 'wi': sd(ks[2], (F, D)), 'wo': sd(ks[3], (D, F)), 'common_wi_a': sd(ks[4], (R_COMMON, D)), 'common_wi_b': sd(ks[5], (F, R_COMMON)), 'common_wo_a': sd(ks[6], (R_COMMON, F)), 'common_wo_b': sd(ks[7], (D, R_COMMON)), 'experts_wi_a': sd(ks[8], (E, R_DOMAIN, D)), 'experts_wi_b': sd(ks[9], (F, R_DOMAIN)) * jnp.ones((E, 1, 1)) * 0.0 + sd(ks[9], (E, F, R_DOMAIN)), 'experts_wo_a': sd(ks[10], (E, R_DOMAIN, F)), 'experts_wo_b': sd(ks[11], (E, D, R_DOMAIN))}
    _L3_cond_all = _L3_cond_setup()
    _L3_cond_in = {k: v for k, v in _L3_cond_all.items() if k in ('wi', 'wo', 'common_wi_a', 'common_wi_b', 'common_wo_a', 'common_wo_b', 'experts_wi_a', 'experts_wi_b', 'experts_wo_a', 'experts_wo_b')}
    del _L3_cond_all
    return {'x': x, 'itok_B_0_63': itok_B_0_63, 'itok_B_0_2': itok_B_0_2, 'itok_B_0_7': itok_B_0_7, 'L0_cond_W': _L0_cond_in['W'], 'L0_cond_b': _L0_cond_in['b'], 'L1_cond_W1': _L1_cond_in['W1'], 'L1_cond_b1': _L1_cond_in['b1'], 'L1_cond_v': _L1_cond_in['v'], 'L2_cond_weight': _L2_cond_in['weight'], 'L2_cond_bias': _L2_cond_in['bias'], 'L3_cond_wi': _L3_cond_in['wi'], 'L3_cond_wo': _L3_cond_in['wo'], 'L3_cond_common_wi_a': _L3_cond_in['common_wi_a'], 'L3_cond_common_wi_b': _L3_cond_in['common_wi_b'], 'L3_cond_common_wo_a': _L3_cond_in['common_wo_a'], 'L3_cond_common_wo_b': _L3_cond_in['common_wo_b'], 'L3_cond_experts_wi_a': _L3_cond_in['experts_wi_a'], 'L3_cond_experts_wi_b': _L3_cond_in['experts_wi_b'], 'L3_cond_experts_wo_a': _L3_cond_in['experts_wo_a'], 'L3_cond_experts_wo_b': _L3_cond_in['experts_wo_b']}

def reference(x, itok_B_0_63, itok_B_0_2, itok_B_0_7, L0_cond_W, L0_cond_b, L1_cond_W1, L1_cond_b1, L1_cond_v, L2_cond_weight, L2_cond_bias, L3_cond_wi, L3_cond_wo, L3_cond_common_wi_a, L3_cond_common_wi_b, L3_cond_common_wo_a, L3_cond_common_wo_b, L3_cond_experts_wi_a, L3_cond_experts_wi_b, L3_cond_experts_wo_a, L3_cond_experts_wo_b):
    import jax
    import jax.numpy as jnp

    def _L0_cond_ref(x, cat_ids, W, b):
        import jax, jax.numpy as jnp
        import numpy as np
        NUM_CATEGORIES = 64
        INPUT_DIM = 128
        HIDDEN_DIM = 128
        B = 32
        S = 64
        selected_W = W[cat_ids]
        selected_b = b[cat_ids]
        out = jnp.einsum('bsd,bdh->bsh', x, selected_W) + selected_b[:, None, :]
        return out

    def _L1_cond_ref(hidden, W1, b1, v, prompt_type_ids):
        import jax, jax.numpy as jnp
        import numpy as np
        NEG_INF = -1e+30
        B, S, D = hidden.shape
        attn_in = jnp.tanh(jnp.einsum('bsd,da->bsa', hidden, W1) + b1)
        scores = jnp.einsum('bsa,a->bs', attn_in, v)
        idx = jnp.arange(S)
        j = idx[:, None]
        l = idx[None, :]
        prefix_m = l <= j
        postfix_m = l >= j
        cloze_m = l != j
        pt = prompt_type_ids[:, None, None]
        mask = jnp.where(pt == 0, prefix_m[None], jnp.where(pt == 1, postfix_m[None], cloze_m[None]))
        masked_scores = jnp.where(mask, scores[:, None, :], NEG_INF)
        p = jax.nn.softmax(masked_scores, axis=-1)
        cnt = jnp.sum(mask, axis=-1).astype(hidden.dtype)
        pooled = jnp.einsum('bjl,bld->bjd', p, hidden) / cnt[..., None]
        return pooled

    def _L2_cond_ref(x, subject_id, weight, bias):
        import jax, jax.numpy as jnp
        import numpy as np
        S, O, H = (8, 128, 128)
        B, N = (32, 64)
        W = weight[subject_id]
        b = bias[subject_id]
        y = jnp.einsum('bnh,boh->bno', x, W) + b[:, None, :]
        return y

    def _L3_cond_ref(hidden_states, expert_ids, wi, wo, common_wi_a, common_wi_b, common_wo_a, common_wo_b, experts_wi_a, experts_wi_b, experts_wo_a, experts_wo_b):
        import jax, jax.numpy as jnp
        import numpy as np
        B, S, D, F = (32, 64, 128, 512)
        R_COMMON, R_DOMAIN, E = (16, 16, 8)
        ALPHA = 2.0

        def _expert_lora(x, expert_ids, Wa, Wb):
            Ab = Wa[expert_ids]
            Bb = Wb[expert_ids]
            low = jnp.einsum('bsd,brd->bsr', x, Ab)
            return ALPHA * jnp.einsum('bsr,bor->bso', low, Bb)
        x = hidden_states
        hidden_i = jnp.einsum('bsd,fd->bsf', x, wi)
        hidden_i += ALPHA * jnp.einsum('bsr,fr->bsf', jnp.einsum('bsd,rd->bsr', x, common_wi_a), common_wi_b)
        hidden_i += _expert_lora(x, expert_ids, experts_wi_a, experts_wi_b)
        hidden_i = jax.nn.relu(hidden_i)
        hidden_o = jnp.einsum('bsf,df->bsd', hidden_i, wo)
        hidden_o += ALPHA * jnp.einsum('bsr,dr->bsd', jnp.einsum('bsf,rf->bsr', hidden_i, common_wo_a), common_wo_b)
        hidden_o += _expert_lora(hidden_i, expert_ids, experts_wo_a, experts_wo_b)
        return hidden_o
    x = x + _L0_cond_ref(x, itok_B_0_63, L0_cond_W, L0_cond_b)
    x = x + _L1_cond_ref(x, L1_cond_W1, L1_cond_b1, L1_cond_v, itok_B_0_2)
    x = x + _L2_cond_ref(x, itok_B_0_7, L2_cond_weight, L2_cond_bias)
    x = x + _L3_cond_ref(x, itok_B_0_7, L3_cond_wi, L3_cond_wo, L3_cond_common_wi_a, L3_cond_common_wi_b, L3_cond_common_wo_a, L3_cond_common_wo_b, L3_cond_experts_wi_a, L3_cond_experts_wi_b, L3_cond_experts_wo_a, L3_cond_experts_wo_b)
    return x

_drawn_inputs = setup_inputs


def setup_inputs(seed=0):
    import zlib

    import numpy as np

    out = dict(_drawn_inputs(seed))
    spreads = {'L0_cond_b': (0.0, 0.1)}
    factors = {}
    for name, (base, spread) in spreads.items():
        noise = np.random.default_rng([zlib.crc32(name.encode()), seed]).standard_normal(out[name].shape)
        drawn = base * np.exp(spread * noise) if base else spread * noise
        out[name] = jnp.asarray(drawn.astype(out[name].dtype))
    for name, factor in factors.items():
        out[name] = (out[name] * factor).astype(out[name].dtype)
    return out
```

```python
from contextlib import ExitStack

import concourse.bass as bass
from concourse import mybir

F32 = mybir.dt.float32
F32R = mybir.dt.float32r
I32 = mybir.dt.int32
ALU = mybir.AluOpType
ACT = mybir.ActivationFunctionType
AX_X = mybir.AxisListType.X

P = 128
ALPHA = 2.0
NEG_INF = -1e30


def build_program(nc, x, cat_ids, type_ids, expert_ids, W0, b0, W1, b1, v, W2, b2, wi, wo,
                  cwi_a, cwi_b, cwo_a, cwo_b, ewi_a, ewi_b, ewo_a, ewo_b, out):
    B, S, D = x.shape
    NCAT = W0.shape[0]
    A = W1.shape[1]
    E = W2.shape[0]
    F = wi.shape[0]
    R = cwi_a.shape[0]
    Q = P // S
    NT = B // Q
    NG = NT // 2
    GB = 2 * Q
    HT = NT // 2
    HB = B // 2
    HN = HT * P
    NC = F // P
    assert D == P and S == 32 and A == 32 and E * R == P and HN == 512 and NT == 8 and NC == 4
    KB = NCAT + E
    DYN = 4
    PG = 2

    with ExitStack() as ctx:
        def sb(name, shape, dt=F32):
            return ctx.enter_context(nc.sbuf_tensor(name, shape, dt))

        def sem(name):
            return ctx.enter_context(nc.semaphore(name))

        bank = [ctx.enter_context(nc.psum_tensor(f"bank{i}", [P, 512], F32)) for i in range(8)]
        TURN = [bank[0], bank[1], bank[0], bank[1]]
        MIX = [bank[2], bank[3], bank[2], bank[2]]
        LOW2, OUT = bank[3], bank[4]
        RING = [bank[5], bank[6], bank[7]]

        ident = sb("ident", [P, P])
        quad = sb("quad", [P, Q, S])
        dist_all = sb("dist_all", [P, Q, S])
        dist_own = sb("dist_own", [P, Q, S])
        dist = sb("dist", [P, S])
        prow = sb("prow", [P, 1])
        krow = sb("krow", [KB, 1])
        oh_ids = sb("oh_ids", [KB, B], I32)
        oh_idf = sb("oh_idf", [KB, B])
        onehot = sb("onehot", [KB, NT, Q, S])
        ty_ids = sb("ty_ids", [P, B], I32)
        ty_f = sb("ty_f", [P, NT, Q])
        ty_own = sb("ty_own", [P, NT, Q])
        ty = sb("ty", [P, NT])
        is_ty = sb("is_ty", [P, 3, NT])
        hide = sb("hide", [P, 3, S])
        seen = sb("seen", [P, 2])
        hide_a = sb("hide_a", [P, NT, S])
        hide_b = sb("hide_b", [P, NT, S])
        hide_c = sb("hide_c", [P, NT, S])
        hide_ab = sb("hide_ab", [P, NT, S])
        mask = sb("mask", [P, NT, S])
        cnt_a = sb("cnt_a", [P, NT])
        cnt_b = sb("cnt_b", [P, NT])
        cnt = sb("cnt", [P, NT])
        ex_ids = sb("ex_ids", [P, B], I32)
        ex_f = sb("ex_f", [P, B])
        ex_off = sb("ex_off", [P, B])
        ex_le = sb("ex_le", [P, B])
        ex_mask = sb("ex_mask", [P, B])
        bias_rows = sb("bias_rows", [KB, 2 * D])
        w0_sb = sb("w0_sb", [P, B, D])
        w1_sb = sb("w1_sb", [P, A])
        b1_sb = sb("b1_sb", [P, 1])
        v_sb = sb("v_sb", [P, 1])
        v_blocks = sb("v_blocks", [P, Q, S])
        w2_nat = sb("w2_nat", [P, E, D])
        w2_t = sb("w2_t", [P, E, D])
        w2_sel = sb("w2_sel", [P, B, D])
        wi_nat = sb("wi_nat", [P, NC, D])
        wo_nat = sb("wo_nat", [P, P, NC])
        cwi_a_sb = sb("cwi_a_sb", [R, D])
        cwi_b_nat = sb("cwi_b_nat", [P, NC, R])
        cwo_a_sb = sb("cwo_a_sb", [R, P, NC])
        cwo_b_nat = sb("cwo_b_nat", [P, R])
        ewi_a_nat = sb("ewi_a_nat", [P, D])
        ewi_b_nat = sb("ewi_b_nat", [P, E, NC, R])
        ewi_b_sb = sb("ewi_b_sb", [P, NC, E, R])
        ewo_a_nat = sb("ewo_a_nat", [P, P, NC])
        ewo_b_nat = sb("ewo_b_nat", [P, E, R])
        cb_t = sb("cb_t", [R, NC + 1, P])
        split = {}
        for name, n in (("wi", NC * P), ("ewi_b", NC * P), ("wo", NC * P), ("ewo_a", NC * P), ("small", 2 * P)):
            split[name] = (sb(name + "_hi", [P, n], F32R), sb(name + "_lo", [P, n], F32R))
        x0 = sb("x0", [P, NT, D])
        x0b = sb("x0b", [P, NT, D])
        b2tok = sb("b2tok", [P, NT, D])
        x0_t = sb("x0_t", [P, NT, P])
        x1 = sb("x1", [P, NT, D + 2])
        x1_t = sb("x1_t", [P, NT, P])
        attn = sb("attn", [P, NT, S])
        scores = sb("scores", [P, NT, S])
        top = sb("top", [P, NT])
        below = sb("below", [P, NT, S])
        below_t = sb("below_t", [P, NT, S])
        probs_t = sb("probs_t", [P, NT, S])
        probs_b = sb("probs_b", [P, NT, Q, S])
        den = sb("den", [P, NT])
        rden = sb("rden", [P, NT])
        x2 = sb("x2", [P, NT, D])
        x2b = sb("x2b", [P, NT, D])
        x2_t = sb("x2_t", [P, NT, P])
        x3 = sb("x3", [P, NT, D])
        x3_hi = sb("x3_hi", [P, NT * P], F32R)
        x3_lo = sb("x3_lo", [P, NT * P], F32R)
        low = [[sb(f"low{k}{h}", [P, HN]) for h in range(2)] for k in range(2)]
        low_hi = [[sb(f"low{k}_hi{h}", [P, HN], F32R) for h in range(2)] for k in range(2)]
        low_lo = [[sb(f"low{k}_lo{h}", [P, HN], F32R) for h in range(2)] for k in range(2)]
        hid_hi = [sb(f"hid_hi{c}", [P, HN], F32R) for c in range(NC)]
        hid_lo = [sb(f"hid_lo{c}", [P, HN], F32R) for c in range(NC)]
        mlp_t = [sb(f"mlp_t{h}", [P, HN]) for h in range(2)]
        out_sb = sb("out_sb", [P, NT, D])

        x_in = [sem(f"x_in{h}") for h in range(2)]
        w0_in = [sem(f"w0_in{g}") for g in range(NG)]
        w0_in_pool = [sem(f"w0_in_pool{g}") for g in range(NG)]
        oh_in, ty_in, ex_in, w1_in, b1_in, v_in, w2_in, bias_in = (sem(n) for n in (
            "oh_in", "ty_in", "ex_in", "w1_in", "b1_in", "v_in", "w2_in", "bias_in"))
        wi_in, wo_in, cwi_in, cwo_in, ewi_a_in, ewi_b_in, ewo_a_in, ewo_b_in = (sem(n) for n in (
            "wi_in", "wo_in", "cwi_in", "cwo_in", "ewi_a_in", "ewi_b_in", "ewo_a_in", "ewo_b_in"))
        out_done = sem("out_done")
        ident_zeroed, ident_ready, quad_step, quad_ready, rows_ready, bias_zeroed, ones_ready, x2b_ready = (
            sem(n) for n in ("ident_zeroed", "ident_ready", "quad_step", "quad_ready", "rows_ready",
                             "bias_zeroed", "ones_ready", "x2b_ready"))
        ewi_b_ready = sem("ewi_b_ready")
        x0_turned, x1_turned, x2_turned, x3_turned = (sem(f"x{k}_turned") for k in range(4))
        w2_turned, cb_turned, prep_turned, bias_spread = (sem(n) for n in (
            "w2_turned", "cb_turned", "prep_turned", "bias_spread"))
        l0_done, attn_in, scores_done, pooled, l2_done = (sem(n) for n in (
            "l0_done", "attn_in", "scores_done", "pooled", "l2_done"))
        low_done, hid_done, low2_done, mlp_done, mlp_turned = (sem(n) for n in (
            "low_done", "hid_done", "low2_done", "mlp_done", "mlp_turned"))
        x0_t_ready, x1_t_ready, x2_t_ready, x3_hi_ready = (sem(n) for n in (
            "x0_t_ready", "x1_t_ready", "x2_t_ready", "x3_hi_ready"))
        w2_t_act, w2_sel_act, prep_hi, b2tok_ready, attn_ready, exp_ready = (sem(n) for n in (
            "w2_t_act", "w2_sel_act", "prep_hi", "b2tok_ready", "attn_ready", "exp_ready"))
        low_hi_ready, hid_hi_ready, low2_hi_ready, mlp_copied = (sem(n) for n in (
            "low_hi_ready", "hid_hi_ready", "low2_hi_ready", "mlp_copied"))
        idf_ready, onehot_ready, ex_step, ex_ready, dist_step, dist_ready, ty_step, mask_step = (
            sem(n) for n in ("idf_ready", "onehot_ready", "ex_step", "ex_ready", "dist_step",
                             "dist_ready", "ty_step", "mask_step"))
        mask_ready, cnt_step, cnt_ready, v_ready, cb_ready, prep_lo, x0b_ready = (sem(n) for n in (
            "mask_ready", "cnt_step", "cnt_ready", "v_ready", "cb_ready", "prep_lo", "x0b_ready"))
        w2_t_dve, w2_sel_dve, x1_ready, masked, top_ready, below_ready, below_t_ready = (sem(n) for n in (
            "w2_t_dve", "w2_sel_dve", "x1_ready", "masked", "top_ready", "below_ready", "below_t_ready"))
        probs_ready, den_ready, rden_ready, x2_ready, x3_ready, x3_lo_ready = (sem(n) for n in (
            "probs_ready", "den_ready", "rden_ready", "x2_ready", "x3_ready", "x3_lo_ready"))
        hid_used = sem("hid_used")
        low_m, low_lo_ready, hid_lo_ready, low2_m, low2_lo_ready, out_ready = (sem(n) for n in (
            "low_m", "low_lo_ready", "hid_lo_ready", "low2_m", "low2_lo_ready", "out_ready"))

        def tiles(g):
            return slice(2 * g, 2 * g + 2)

        def group_bank(b, w=P):
            return b[:, 0:2 * w].rearrange("p (t n) -> p t n", t=2)

        x_tok = x.rearrange("b s d -> (b s) d").rearrange("(t p) d -> p t d", p=P)
        out_tok = out.rearrange("b s d -> (b s) d").rearrange("(t p) d -> p t d", p=P)
        cat_row = cat_ids.rearrange("(o b) -> o b", o=1)
        type_row = type_ids.rearrange("(o b) -> o b", o=1)
        expert_row = expert_ids.rearrange("(o b) -> o b", o=1)

        def gather_w0(eng, regs, b_first, n, landed):
            eng.load(regs[:n], cat_row[0:1, b_first:b_first + n])
            for k in range(n):
                cat = eng.snap(regs[k], min_val=0, max_val=NCAT - 1)
                b = b_first + k
                eng.dma_start(w0_sb[:, b, :], W0[bass.ds(cat, 1), :, :].rearrange("o d h -> (o d) h"))\
                   .then_inc(landed[b // GB], 16)

        block = ctx.enter_context(nc.Block())

        @block.sync
        def _(sp):
            regs = [sp.alloc_register(f"sp_cat{k}") for k in range(DYN)]
            sp.dma_start(x0[:, 0:HT, :], x_tok[:, 0:HT, :]).then_inc(x_in[0], 16)
            for g in range(NG):
                gather_w0(sp, regs, GB * g, 4, w0_in)
                gather_w0(sp, regs, GB * g + 4, GB - 4 - PG, w0_in)
                if g == 1:
                    sp.dma_start(x0[:, HT:NT, :], x_tok[:, HT:NT, :]).then_inc(x_in[1], 16)
                    sp.dma_start(wi_nat[:, :, :], wi.rearrange("(p c) d -> p c d", c=NC)).then_inc(wi_in, 16)
                    sp.dma_start(wo_nat[:, :, :], wo.rearrange("d (p c) -> d p c", c=NC)).then_inc(wo_in, 16)
            for h in range(2):
                sp.wait_ge(out_ready, h + 1)
                t = slice(HT * h, HT * h + HT)
                sp.dma_start(out_tok[:, t, :], out_sb[:, t, :]).then_inc(out_done, 16)
            sp.wait_ge(out_done, 32)

        @block.gpsimd
        def _(pool):
            regs = [pool.alloc_register(f"pool_cat{k}") for k in range(PG)]
            pool.memset(ident[:, :], 0.0).then_inc(ident_zeroed, 1)
            pool.wait_ge(ident_zeroed, 1)
            pool.affine_select(out=ident[:, :], in_=ident[:, :], compare_op=ALU.not_equal, fill=1.0, base=0,
                               pattern=[[-1, P]], channel_multiplier=1).then_inc(ident_ready, 1)
            gather_w0(pool, regs, GB - PG, PG, w0_in_pool)
            pool.memset(bias_rows[:, :], 0.0).then_inc(bias_zeroed, 1)
            pool.iota(prow[:, :], [[0, 1]], 0, channel_multiplier=1,
                      allow_small_or_imprecise_dtypes=True).then_inc(rows_ready, 1)
            pool.iota(krow[0:NCAT, :], [[0, 1]], 0, channel_multiplier=1,
                      allow_small_or_imprecise_dtypes=True).then_inc(rows_ready, 1)
            pool.wait_ge(rows_ready, 2)
            pool.iota(krow[NCAT:KB, :], [[0, 1]], 0, channel_multiplier=1,
                      allow_small_or_imprecise_dtypes=True).then_inc(rows_ready, 1)
            pool.wait_ge(rows_ready, 3)
            pool.iota(dist_all[:, :, :], [[S, Q], [1, S]], 0, channel_multiplier=-1,
                      allow_small_or_imprecise_dtypes=True).then_inc(rows_ready, 1)
            pool.memset(quad[:, :, :], 1.0).then_inc(quad_step, 1)
            pool.wait_ge(quad_step, 1)
            pool.affine_select(out=quad[:, :, :], in_=quad[:, :, :], compare_op=ALU.is_ge, fill=0.0, base=0,
                               pattern=[[-S, Q], [0, S]], channel_multiplier=1).then_inc(quad_step, 1)
            pool.wait_ge(quad_step, 2)
            pool.affine_select(out=quad[:, :, :], in_=quad[:, :, :], compare_op=ALU.is_ge, fill=0.0, base=S - 1,
                               pattern=[[S, Q], [0, S]], channel_multiplier=-1).then_inc(quad_ready, 1)
            pool.memset(x1[:, :, D:D + 2], 1.0).then_inc(ones_ready, 1)
            gather_w0(pool, regs, 2 * GB - PG, PG, w0_in_pool)
            pool.dma_start(ewi_b_nat[:, :, :, :], ewi_b.rearrange("e (p c) r -> p e c r", c=NC)).then_inc(ewi_b_in, 16)
            pool.dma_start(ewo_a_nat[:, :, :], ewo_a.rearrange("e r (p c) -> (e r) p c", c=NC)).then_inc(ewo_a_in, 16)
            pool.dma_start(ewo_b_nat[:, :, :], ewo_b.rearrange("e d r -> d e r")).then_inc(ewo_b_in, 16)
            pool.dma_start(cwo_a_sb[:, :, :], cwo_a.rearrange("r (p c) -> r p c", c=NC)).then_inc(cwo_in, 16)
            pool.dma_start(cwo_b_nat[:, :], cwo_b).then_inc(cwo_in, 16)
            for g in range(2, NG):
                gather_w0(pool, regs, GB * g + GB - PG, PG, w0_in_pool)
            pool.wait_ge(ewi_b_in, 16)
            pool.tensor_copy(ewi_b_sb[:, :, :, :].rearrange("p c e r -> p e c r"), ewi_b_nat[:, :, :, :])\
                .then_inc(ewi_b_ready, 1)
            for g in range(NG):
                pool.wait_ge(b2tok_ready, g + 1)
                pool.wait_ge(x2_ready, 2 * (g + 1))
                pool.tensor_tensor(x2b[:, tiles(g), :], x2[:, tiles(g), :], b2tok[:, tiles(g), :],
                                   ALU.add).then_inc(x2b_ready, 1)

        @block.tensor
        def _(pe):
            def turn_x(src, g, b, done):
                for k in range(2):
                    mm = pe.transpose(b[:, k * P:k * P + P], src[:, 2 * g + k, 0:D], ident[:, :])
                mm.then_inc(done, 1)

            def turn_x0(g, b, col):
                if g % 2 == 0:
                    pe.wait_ge(x_in[g // 2], 16)
                for k in range(2):
                    mm = pe.transpose(b[:, col + k * P:col + k * P + P], x0[:, 2 * g + k, :], ident[:, :])
                mm.then_inc(x0_turned, 1)

            def spread_bias(g, b):
                for k in range(2):
                    mm = pe.matmul(b[:, k * 2 * D:(k + 1) * 2 * D],
                                   onehot[:, 2 * g + k, :, :].rearrange("k q s -> k (q s)"),
                                   bias_rows[:, :], start=True, stop=True)
                mm.then_inc(bias_spread, 1)

            def turn_w2(n, b):
                for k in range(4):
                    mm = pe.transpose(b[:, k * P:k * P + P], w2_nat[:, 4 * n + k, :], ident[:, :])
                mm.then_inc(w2_turned, 1)

            def rows_times(src_t, w, g, done):
                for k in range(2):
                    for q in range(Q):
                        t = 2 * g + k
                        mm = pe.matmul(MIX[g][q * S:q * S + S, k * D:k * D + D], src_t[:, t, q * S:q * S + S],
                                       w[:, Q * t + q, :], start=True, stop=True)
                mm.then_inc(done, 1)

            def layer0(g):
                pe.wait_ge(w0_in[g], 16 * (GB - PG))
                pe.wait_ge(w0_in_pool[g], 16 * PG)
                pe.wait_ge(x0_t_ready, g + 1)
                rows_times(x0_t, w0_sb, g, l0_done)

            def turn_x1(g):
                pe.wait_ge(x1_ready, g + 1)
                turn_x(x1, g, TURN[g], x1_turned)

            def attn_product(g):
                pe.wait_ge(x1_t_ready, g + 1)
                for q in range(Q):
                    mm = pe.matmul(MIX[g][q * S:q * S + S, 0:2 * S].rearrange("p (t l) -> p t l", t=2),
                                   w1_sb[:, :], x1_t[:, tiles(g), q * S:q * S + S], start=True, stop=True)
                mm.then_inc(attn_in, 1)

            def score_product(g):
                pe.wait_ge(attn_ready, g + 1)
                for q in range(Q):
                    mm = pe.matmul(MIX[g][q * S:q * S + S, 0:2 * S].rearrange("p (t l) -> p t l", t=2),
                                   v_blocks[:, q, :], attn[:, tiles(g), :], start=True, stop=True)
                mm.then_inc(scores_done, 1)

            def pool_rows(g):
                pe.wait_ge(probs_ready, g + 1)
                pe.wait_ge(ones_ready, 1)
                for k in range(2):
                    mm = pe.matmul(MIX[g][:, 256 * k:256 * k + D + 1],
                                   probs_b[:, 2 * g + k, :, :].rearrange("p q j -> p (q j)"),
                                   x1[:, 2 * g + k, 0:D + 1], start=True, stop=True)
                mm.then_inc(pooled, 1)

            def turn_x2(g):
                pe.wait_ge(x2_ready, 2 * (g + 1))
                turn_x(x2, g, TURN[g], x2_turned)

            def layer2(g):
                pe.wait_ge(x2_t_ready, g + 1)
                pe.wait_ge(w2_sel_act, (g + 1) * GB // 2)
                pe.wait_ge(w2_sel_dve, (g + 1) * GB // 2)
                rows_times(x2_t, w2_sel, g, l2_done)

            def turn_x3(g):
                pe.wait_ge(x3_ready, g + 1)
                turn_x(x3, g, TURN[g], x3_turned)

            def three(acc, w, col, hi, lo, first, last):
                w_hi, w_lo = split[w]
                c = slice(col * P, col * P + P)
                pe.matmul(acc, w_hi[:, c], hi, start=first, stop=False, skip_group_check=True)
                pe.matmul(acc, w_hi[:, c], lo, start=False, stop=False, skip_group_check=True)
                return pe.matmul(acc, w_lo[:, c], hi, start=False, stop=last, skip_group_check=True)

            def ring(h, k):
                return RING[(5 * h + k) % 3][:, :]

            def half(a, h):
                return a[:, HN * h:HN * h + HN]

            def wait_ring(h, k):
                n = 5 * h + k - 3
                if n in (0, 5):
                    pe.wait_ge(low_m, n // 5 + 1)
                elif n > 0:
                    pe.wait_ge(hid_lo_ready, n - n // 5)

            def low_rank(h):
                wait_ring(h, 0)
                pe.wait_ge(x3_hi_ready, 2 * (h + 1))
                pe.wait_ge(x3_lo_ready, 2 * (h + 1))
                three(ring(h, 0), "small", 0, half(x3_hi, h), half(x3_lo, h), True, True).then_inc(low_done, 1)

            def hidden_dense(h, c):
                wait_ring(h, c + 1)
                three(ring(h, c + 1), "wi", c, half(x3_hi, h), half(x3_lo, h), True, False)

            def hidden_low(h, c):
                if c == 0:
                    pe.wait_ge(low_hi_ready, h + 1)
                    pe.wait_ge(low_lo_ready, h + 1)
                three(ring(h, c + 1), "ewi_b", c, low_hi[0][h][:, :], low_lo[0][h][:, :], False, True)\
                    .then_inc(hid_done, 1)

            def out_low(h, c):
                pe.wait_ge(hid_hi_ready, 4 * h + c + 1)
                pe.wait_ge(hid_lo_ready, 4 * h + c + 1)
                if c == 0 and h == 1:
                    pe.wait_ge(low2_m, 1)
                mm = three(LOW2[:, :], "ewo_a", c, hid_hi[c][:, :], hid_lo[c][:, :], c == 0, c == NC - 1)
                if c == NC - 1:
                    mm.then_inc(low2_done, 1)

            def out_dense(h, c):
                if c == 0 and h == 1:
                    pe.wait_ge(out_ready, 1)
                mm = three(OUT[:, :], "wo", c, hid_hi[c][:, :], hid_lo[c][:, :], c == 0, False)
                mm.then_inc(hid_used, 1)

            def out_expert(h):
                pe.wait_ge(low2_hi_ready, h + 1)
                pe.wait_ge(low2_lo_ready, h + 1)
                three(OUT[:, :], "small", 1, low_hi[1][h][:, :], low_lo[1][h][:, :], False, True)\
                    .then_inc(mlp_done, 1)

            def turn_mlp(h):
                pe.wait_ge(mlp_copied, h + 1)
                for k in range(HT):
                    mm = pe.transpose(OUT[:, k * P:k * P + P], mlp_t[h][:, k * P:k * P + P], ident[:, :])
                mm.then_inc(mlp_turned, 1)

            pe.wait_ge(ident_ready, 1)
            turn_x0(0, bank[5], 0)
            turn_x0(1, bank[4], 0)
            pe.wait_ge(w2_in, 16)
            turn_w2(0, bank[6])
            turn_w2(1, bank[7])
            pe.wait_ge(onehot_ready, 2)
            pe.wait_ge(bias_in, 32)
            spread_bias(0, bank[0])
            spread_bias(1, bank[1])
            layer0(0)
            pe.wait_ge(cwi_in, 32)
            pe.wait_ge(ewi_a_in, 16)
            pe.wait_ge(x0b_ready, 2)
            pe.wait_ge(b2tok_ready, 2)
            turn_x1(0)
            attn_product(0)
            layer0(1)
            pe.wait_ge(x0_t_ready, 2)
            for c in range(NC):
                mm = pe.transpose(bank[4][0:R, c * P:c * P + P], cwi_b_nat[:, c, :], ident[:, :])
            mm.then_inc(cb_turned, 1)
            score_product(0)
            turn_x1(1)
            attn_product(1)
            pe.wait_ge(x_in[1], 16)
            turn_x0(2, bank[5], 0)
            turn_x0(3, bank[5], 256)
            score_product(1)
            pe.wait_ge(wi_in, 16)
            pe.wait_ge(cb_ready, 1)
            pe.wait_ge(w2_t_act, 1)
            for c in range(NC):
                pe.matmul(bank[6][:, c * P:c * P + P], wi_nat[:, c, :], ident[:, :], start=True, stop=False)
                mm = pe.matmul(bank[6][:, c * P:c * P + P], cwi_a_sb[:, :], cb_t[:, c, :], start=False, stop=True)
            mm.then_inc(prep_turned, 1)
            pool_rows(0)
            pe.wait_ge(ewi_b_ready, 1)
            pe.wait_ge(w2_t_dve, 1)
            for c in range(NC):
                mm = pe.transpose(bank[7][:, c * P:c * P + P], ewi_b_sb[:, c, :, :].rearrange("p e r -> p (e r)"), ident[:, :])
            mm.then_inc(prep_turned, 1)
            turn_x2(0)
            pool_rows(1)
            pe.wait_ge(ewo_b_in, 16)
            pe.wait_ge(cwo_in, 32)
            pe.transpose(bank[4][:, 0:P], ewi_a_nat[:, :], ident[:, :])
            pe.transpose(bank[4][:, P:2 * P], ewo_b_nat[:, :, :].rearrange("p e r -> p (e r)"), ident[:, :])
            pe.transpose(bank[4][0:R, 2 * P:3 * P], cwo_b_nat[:, :], ident[:, :]).then_inc(prep_turned, 1)
            layer2(0)
            turn_x2(1)
            pe.wait_ge(ewo_a_in, 16)
            pe.wait_ge(x0_t_ready, 4)
            for c in range(NC):
                mm = pe.transpose(bank[5][:, c * P:c * P + P], ewo_a_nat[:, :, c], ident[:, :])
            mm.then_inc(prep_turned, 1)
            layer2(1)
            turn_x3(0)
            pe.wait_ge(wo_in, 16)
            pe.wait_ge(cb_ready, 2)
            pe.wait_ge(prep_lo, 3)
            for c in range(NC):
                pe.matmul(bank[4][:, c * P:c * P + P], wo_nat[:, :, c], ident[:, :], start=True, stop=False)
                mm = pe.matmul(bank[4][:, c * P:c * P + P], cwo_a_sb[:, :, c], cb_t[:, NC, :], start=False, stop=True)
            mm.then_inc(prep_turned, 1)
            turn_x3(1)
            pe.wait_ge(prep_lo, 5)
            low_rank(0)
            hidden_dense(0, 0)
            hidden_dense(0, 1)
            pe.wait_ge(x3_lo_ready, 2)
            pe.wait_ge(onehot_ready, 2)
            spread_bias(2, bank[0])
            spread_bias(3, bank[1])
            layer0(2)
            hidden_low(0, 0)
            hidden_low(0, 1)
            pe.wait_ge(x1_ready, 3)
            layer0(3)
            hidden_dense(0, 2)
            hidden_low(0, 2)
            pe.wait_ge(x0b_ready, 4)
            pe.wait_ge(b2tok_ready, 4)
            turn_x1(2)
            out_low(0, 0)
            out_dense(0, 0)
            turn_x1(3)
            attn_product(2)
            hidden_dense(0, 3)
            hidden_low(0, 3)
            pe.wait_ge(attn_ready, 3)
            attn_product(3)
            out_low(0, 1)
            pe.wait_ge(attn_ready, 4)
            score_product(2)
            out_dense(0, 1)
            pe.wait_ge(masked, 3)
            score_product(3)
            out_low(0, 2)
            out_low(0, 3)
            pe.wait_ge(masked, 4)
            pool_rows(2)
            out_dense(0, 2)
            pe.wait_ge(x2_ready, 6)
            pool_rows(3)
            turn_x2(2)
            out_dense(0, 3)
            pe.wait_ge(x2_ready, 8)
            layer2(2)
            turn_x2(3)
            out_expert(0)
            pe.wait_ge(x3_ready, 3)
            layer2(3)
            turn_x3(2)
            turn_x3(3)
            turn_mlp(0)
            low_rank(1)
            for c in range(2):
                hidden_dense(1, c)
            for c in range(2):
                hidden_low(1, c)
            hidden_dense(1, 2)
            hidden_low(1, 2)
            out_low(1, 0)
            out_dense(1, 0)
            hidden_dense(1, 3)
            hidden_low(1, 3)
            out_low(1, 1)
            out_low(1, 2)
            out_dense(1, 1)
            out_low(1, 3)
            out_dense(1, 2)
            out_dense(1, 3)
            out_expert(1)
            turn_mlp(1)

        @block.scalar
        def _(act):
            regs = [act.alloc_register(f"act_ex{k}") for k in range(DYN)]

            def copy_turned(dst, b, g, col, turned, ready):
                act.wait_ge(turned, g + 1)
                act.copy(dst[:, tiles(g), :].rearrange("p t n -> p (t n)"), b[:, col:col + 2 * P]).then_inc(ready, 1)

            def select_w2(g):
                act.load(regs, expert_row[0:1, GB * g:GB * g + DYN])
                for k in range(DYN):
                    e = act.snap(regs[k], min_val=0, max_val=E - 1)
                    act.copy(w2_sel[:, GB * g + k, :], w2_t[:, bass.ds(e, 1), :].rearrange("p o n -> p (o n)"))\
                       .then_inc(w2_sel_act, 1)

            def keep_b2(g, b):
                act.wait_ge(x0b_ready, g + 1)
                act.copy(b2tok[:, tiles(g), :], b[:, :].rearrange("p (t n) -> p t n", t=2)[:, :, D:2 * D])\
                   .then_inc(b2tok_ready, 1)

            def attn_tanh(g):
                act.wait_ge(attn_in, g + 1)
                act.activation(attn[:, tiles(g), :].rearrange("p t l -> p (t l)"), MIX[g][:, 0:2 * S], ACT.Tanh,
                               bias=b1_sb[:, :]).then_inc(attn_ready, 1)

            def exp_scores(g):
                act.wait_ge(below_t_ready, g + 1)
                act.activation(probs_t[:, tiles(g), :].rearrange("p t l -> p (t l)"),
                               below_t[:, tiles(g), :].rearrange("p t l -> p (t l)"), ACT.Exp).then_inc(exp_ready, 1)

            def x3_high(g):
                act.wait_ge(x3_turned, g + 1)
                act.copy(x3_hi[:, 2 * P * g:2 * P * (g + 1)], TURN[g][:, 0:2 * P]).then_inc(x3_hi_ready, 1)

            def prep_high(n, w, b, width):
                act.wait_ge(prep_turned, n + 1)
                act.copy(split[w][0][:, :], b[:, 0:width]).then_inc(prep_hi, 1)

            def low_high(k, h, m, ready):
                act.wait_ge(m, h + 1)
                act.copy(low_hi[k][h][:, :], low[k][h][:, :]).then_inc(ready, 1)

            def hidden_high(h, c):
                act.wait_ge(hid_done, 4 * h + c + 1)
                if h == 1:
                    act.wait_ge(hid_used, c + 1)
                act.activation(hid_hi[c][:, :], RING[(5 * h + c + 1) % 3][:, :], ACT.Relu).then_inc(hid_hi_ready, 1)

            def copy_mlp(h):
                act.wait_ge(mlp_done, h + 1)
                act.copy(mlp_t[h][:, :], OUT[:, :]).then_inc(mlp_copied, 1)

            act.dma_start(oh_ids[0:NCAT, :], cat_row.partition_broadcast(NCAT)).then_inc(oh_in, 16)
            act.dma_start(oh_ids[NCAT:KB, :], expert_row.partition_broadcast(E)).then_inc(oh_in, 16)
            act.dma_start(w2_nat[:, :, :], W2.rearrange("e o h -> o e h")).then_inc(w2_in, 16)
            act.wait_ge(bias_zeroed, 1)
            act.dma_start(bias_rows[0:NCAT, 0:D], b0).then_inc(bias_in, 16)
            act.dma_start(bias_rows[NCAT:KB, D:2 * D], b2).then_inc(bias_in, 16)
            act.dma_start(w1_sb[:, :], W1).then_inc(w1_in, 16)
            for q in range(Q):
                act.dma_start(b1_sb[q * S:q * S + S, :], b1.rearrange("(a o) -> a o", o=1)).then_inc(b1_in, 16)
                act.dma_start(v_sb[q * S:q * S + S, :], v.rearrange("(a o) -> a o", o=1)).then_inc(v_in, 16)
            act.dma_start(ty_ids[:, :], type_row.partition_broadcast(P)).then_inc(ty_in, 16)
            act.dma_start(ex_ids[:, :], expert_row.partition_broadcast(P)).then_inc(ex_in, 16)
            act.dma_start(cwi_a_sb[:, :], cwi_a).then_inc(cwi_in, 16)
            act.dma_start(cwi_b_nat[:, :, :], cwi_b.rearrange("(p c) r -> p c r", c=NC)).then_inc(cwi_in, 16)
            act.dma_start(ewi_a_nat[:, :], ewi_a.rearrange("e r d -> (e r) d")).then_inc(ewi_a_in, 16)

            copy_turned(x0_t, bank[5], 0, 0, x0_turned, x0_t_ready)
            copy_turned(x0_t, bank[4], 1, 0, x0_turned, x0_t_ready)
            act.wait_ge(w2_turned, 1)
            act.copy(w2_t[:, 0:4, :].rearrange("p e n -> p (e n)"), bank[6][:, :]).then_inc(w2_t_act, 1)
            keep_b2(0, bank[0])
            keep_b2(1, bank[1])
            act.wait_ge(w2_t_act, 1)
            act.wait_ge(w2_t_dve, 1)
            select_w2(0)
            copy_turned(x1_t, TURN[0], 0, 0, x1_turned, x1_t_ready)
            act.wait_ge(b1_in, 64)
            attn_tanh(0)
            select_w2(1)
            copy_turned(x1_t, TURN[1], 1, 0, x1_turned, x1_t_ready)
            attn_tanh(1)
            act.wait_ge(x0_turned, 4)
            copy_turned(x0_t, bank[5], 2, 0, x0_turned, x0_t_ready)
            copy_turned(x0_t, bank[5], 3, 256, x0_turned, x0_t_ready)
            exp_scores(0)
            prep_high(0, "wi", bank[6], NC * P)
            exp_scores(1)
            prep_high(1, "ewi_b", bank[7], NC * P)
            copy_turned(x2_t, TURN[0], 0, 0, x2_turned, x2_t_ready)
            prep_high(2, "small", bank[4], 2 * P)
            copy_turned(x2_t, TURN[1], 1, 0, x2_turned, x2_t_ready)
            prep_high(3, "ewo_a", bank[5], NC * P)
            x3_high(0)
            x3_high(1)
            prep_high(4, "wo", bank[4], NC * P)
            select_w2(2)
            select_w2(3)
            low_high(0, 0, low_m, low_hi_ready)
            keep_b2(2, bank[0])
            keep_b2(3, bank[1])
            hidden_high(0, 0)
            hidden_high(0, 1)
            copy_turned(x1_t, TURN[2], 2, 0, x1_turned, x1_t_ready)
            hidden_high(0, 2)
            copy_turned(x1_t, TURN[3], 3, 0, x1_turned, x1_t_ready)
            attn_tanh(2)
            hidden_high(0, 3)
            attn_tanh(3)
            exp_scores(2)
            exp_scores(3)
            copy_turned(x2_t, TURN[2], 2, 0, x2_turned, x2_t_ready)
            low_high(1, 0, low2_m, low2_hi_ready)
            copy_turned(x2_t, TURN[3], 3, 0, x2_turned, x2_t_ready)
            copy_mlp(0)
            x3_high(2)
            x3_high(3)
            low_high(0, 1, low_m, low_hi_ready)
            for c in range(NC):
                hidden_high(1, c)
            low_high(1, 1, low2_m, low2_hi_ready)
            copy_mlp(1)

        @block.vector
        def _(dve):
            regs = [dve.alloc_register(f"dve_ex{k}") for k in range(DYN)]

            def select_w2(g):
                first = GB * g + DYN
                dve.load(regs, expert_row[0:1, first:first + DYN])
                for k in range(DYN):
                    e = dve.snap(regs[k], min_val=0, max_val=E - 1)
                    dve.tensor_copy(w2_sel[:, first + k, :], w2_t[:, bass.ds(e, 1), :].rearrange("p o n -> p (o n)"))\
                       .then_inc(w2_sel_dve, 1)

            def add_b0(g, b):
                dve.wait_ge(x_in[g // 2], 16)
                dve.wait_ge(bias_spread, g + 1)
                dve.tensor_tensor(x0b[:, tiles(g), :], b[:, :].rearrange("p (t n) -> p t n", t=2)[:, :, 0:D],
                                  x0[:, tiles(g), :], ALU.add).then_inc(x0b_ready, 1)

            def make_x1(g):
                dve.wait_ge(l0_done, g + 1)
                dve.wait_ge(x0b_ready, g + 1)
                dve.tensor_tensor(x1[:, tiles(g), 0:D], group_bank(MIX[g]), x0b[:, tiles(g), :], ALU.add)\
                   .then_inc(x1_ready, 1)

            def below_top(g):
                t = tiles(g)
                dve.wait_ge(scores_done, g + 1)
                dve.tensor_tensor(scores[:, t, :], group_bank(MIX[g], S), mask[:, t, :], ALU.add).then_inc(masked, 1)
                dve.wait_ge(masked, g + 1)
                dve.tensor_reduce(top[:, t], scores[:, t, :], AX_X, ALU.max).then_inc(top_ready, 1)
                dve.wait_ge(top_ready, g + 1)
                dve.tensor_tensor(below[:, t, :], scores[:, t, :], top[:, t].unsqueeze(2).to_broadcast([P, 2, S]),
                                  ALU.subtract).then_inc(below_ready, 1)
                dve.wait_ge(below_ready, g + 1)
                dve.transpose(below_t[:, t, :].rearrange("p t l -> p (t l)"),
                              below[:, t, :].rearrange("p t l -> p (t l)")).then_inc(below_t_ready, 1)

            def block_probs(g):
                dve.wait_ge(exp_ready, g + 1)
                for k in range(2):
                    ins = dve.tensor_tensor(probs_b[:, 2 * g + k, :, :],
                                            probs_t[:, 2 * g + k, :].unsqueeze(1).to_broadcast([P, Q, S]),
                                            quad[:, :, :], ALU.mult)
                ins.then_inc(probs_ready, 1)

            def make_x2(g):
                t = tiles(g)
                dve.wait_ge(pooled, g + 1)
                dve.tensor_tensor(den[:, t], MIX[g][:, :].rearrange("p (t n) -> p t n", t=2)[:, :, D],
                                  cnt[:, t], ALU.mult).then_inc(den_ready, 1)
                dve.wait_ge(den_ready, g + 1)
                dve.reciprocal(rden[:, t], den[:, t]).then_inc(rden_ready, 1)
                dve.wait_ge(rden_ready, g + 1)
                for k in range(2):
                    dve.scalar_tensor_tensor(out=x2[:, 2 * g + k, :], in0=MIX[g][:, 256 * k:256 * k + D],
                                             scalar=rden[:, 2 * g + k:2 * g + k + 1], in1=x1[:, 2 * g + k, 0:D],
                                             op0=ALU.mult, op1=ALU.add).then_inc(x2_ready, 1)

            def make_x3(g):
                dve.wait_ge(l2_done, g + 1)
                dve.wait_ge(x2b_ready, g + 1)
                dve.tensor_tensor(x3[:, tiles(g), :], group_bank(MIX[g]), x2b[:, tiles(g), :], ALU.add)\
                   .then_inc(x3_ready, 1)

            def x3_low(g):
                c = slice(2 * P * g, 2 * P * (g + 1))
                dve.wait_ge(x3_hi_ready, g + 1)
                dve.tensor_tensor(x3_lo[:, c], TURN[g][:, 0:2 * P], x3_hi[:, c].bitcast(F32), ALU.subtract)\
                   .then_inc(x3_lo_ready, 1)

            def prep_low(n, w, b, width):
                dve.wait_ge(prep_hi, n + 1)
                dve.tensor_tensor(split[w][1][:, :], b[:, 0:width], split[w][0][:, :].bitcast(F32), ALU.subtract)\
                   .then_inc(prep_lo, 1)

            def mask_low(k, h, b, done, m):
                dve.wait_ge(done, h + 1)
                dve.tensor_tensor(low[k][h][:, :].rearrange("p (b s) -> p b s", s=S),
                                  b[:, :].rearrange("p (b s) -> p b s", s=S),
                                  ex_mask[:, HB * h:HB * h + HB].unsqueeze(2).to_broadcast([P, HB, S]), ALU.mult)\
                   .then_inc(m, 1)

            def low_low(k, h, hi_ready, ready):
                dve.wait_ge(hi_ready, h + 1)
                dve.tensor_tensor(low_lo[k][h][:, :], low[k][h][:, :], low_hi[k][h][:, :].bitcast(F32), ALU.subtract)\
                   .then_inc(ready, 1)

            def hidden_lo(h, c):
                dve.wait_ge(hid_hi_ready, 4 * h + c + 1)
                dve.scalar_tensor_tensor(out=hid_lo[c][:, :], in0=RING[(5 * h + c + 1) % 3][:, :], scalar=0.0,
                                         in1=hid_hi[c][:, :].bitcast(F32), op0=ALU.max, op1=ALU.subtract)\
                   .then_inc(hid_lo_ready, 1)

            def finish(h):
                t = slice(HT * h, HT * h + HT)
                dve.wait_ge(mlp_turned, h + 1)
                dve.tensor_tensor(out_sb[:, t, :], OUT[:, :].rearrange("p (t n) -> p t n", t=HT), x3[:, t, :],
                                  ALU.add).then_inc(out_ready, 1)

            dve.wait_ge(oh_in, 32)
            dve.tensor_copy(oh_idf[:, :], oh_ids[:, :]).then_inc(idf_ready, 1)
            dve.wait_ge(idf_ready, 1)
            dve.wait_ge(rows_ready, 4)
            for h in range(2):
                dve.tensor_scalar(onehot[:, HT * h:HT * h + HT, :, :].rearrange("p t q s -> p (t q) s"),
                                  oh_idf[:, HB * h:HB * h + HB].unsqueeze(2).to_broadcast([KB, HB, S]),
                                  krow[:, :], None, ALU.is_equal).then_inc(onehot_ready, 1)
            add_b0(0, bank[0])
            add_b0(1, bank[1])
            dve.wait_ge(w2_turned, 2)
            dve.tensor_copy(w2_t[:, 4:8, :].rearrange("p e n -> p (e n)"), bank[7][:, :]).then_inc(w2_t_dve, 1)
            dve.wait_ge(quad_ready, 1)
            dve.wait_ge(v_in, 64)
            dve.tensor_scalar(v_blocks[:, :, :], quad[:, :, :], v_sb[:, :], None, ALU.mult).then_inc(v_ready, 1)
            dve.tensor_tensor(dist_own[:, :, :], dist_all[:, :, :], quad[:, :, :], ALU.mult).then_inc(dist_step, 1)
            dve.wait_ge(dist_step, 1)
            dve.tensor_reduce(dist[:, :], dist_own[:, :, :].rearrange("p q l -> p l q"), AX_X, ALU.add)\
               .then_inc(dist_ready, 1)
            dve.wait_ge(ty_in, 16)
            dve.tensor_copy(ty_f[:, :, :].rearrange("p t q -> p (t q)"), ty_ids[:, :]).then_inc(ty_step, 1)
            dve.wait_ge(ty_step, 1)
            dve.tensor_tensor(ty_own[:, :, :], ty_f[:, :, :], quad[:, :, 0].unsqueeze(1).to_broadcast([P, NT, Q]),
                              ALU.mult).then_inc(ty_step, 1)
            dve.wait_ge(ty_step, 2)
            dve.tensor_reduce(ty[:, :], ty_own[:, :, :], AX_X, ALU.add).then_inc(ty_step, 1)
            dve.wait_ge(dist_ready, 1)
            for n, op in enumerate((ALU.is_gt, ALU.is_lt, ALU.is_equal)):
                dve.tensor_scalar(hide[:, n, :], dist[:, :], 0.0, NEG_INF, op, ALU.mult).then_inc(mask_step, 1)
            dve.tensor_scalar(seen[:, 0:1], dist[:, 0:1], -1.0, 1.0, ALU.mult, ALU.add).then_inc(cnt_step, 1)
            dve.tensor_scalar(seen[:, 1:2], dist[:, 0:1], float(S), None, ALU.add).then_inc(cnt_step, 1)
            dve.wait_ge(ty_step, 3)
            dve.tensor_scalar(is_ty[:, 0, :], ty[:, :], 0.0, None, ALU.is_equal).then_inc(ty_step, 1)
            dve.tensor_scalar(is_ty[:, 1, :], ty[:, :], 1.0, None, ALU.is_equal).then_inc(ty_step, 1)
            dve.wait_ge(ty_step, 5)
            dve.scalar_tensor_tensor(out=cnt_a[:, :], in0=is_ty[:, 0, :], scalar=1.0, in1=is_ty[:, 1, :],
                                     op0=ALU.mult, op1=ALU.add).then_inc(ty_step, 1)
            dve.wait_ge(ty_step, 6)
            dve.tensor_scalar(is_ty[:, 2, :], cnt_a[:, :], -1.0, 1.0, ALU.mult, ALU.add).then_inc(ty_step, 1)
            dve.wait_ge(ty_step, 7)
            dve.wait_ge(mask_step, 3)
            for n, part in enumerate((hide_a, hide_b, hide_c)):
                dve.tensor_tensor(part[:, :, :], is_ty[:, n, :].unsqueeze(2).to_broadcast([P, NT, S]),
                                  hide[:, n, :].unsqueeze(1).to_broadcast([P, NT, S]), ALU.mult).then_inc(mask_step, 1)
            dve.wait_ge(mask_step, 5)
            dve.tensor_tensor(hide_ab[:, :, :], hide_a[:, :, :], hide_b[:, :, :], ALU.add).then_inc(mask_step, 1)
            dve.wait_ge(mask_step, 7)
            dve.tensor_tensor(mask[:, :, :], hide_ab[:, :, :], hide_c[:, :, :], ALU.add).then_inc(mask_ready, 1)
            make_x1(0)
            dve.wait_ge(cnt_step, 2)
            dve.tensor_scalar(cnt_b[:, :], is_ty[:, 0, :], seen[:, 0:1], None, ALU.mult).then_inc(cnt_step, 1)
            dve.wait_ge(cnt_step, 3)
            dve.scalar_tensor_tensor(out=cnt_a[:, :], in0=is_ty[:, 1, :], scalar=seen[:, 1:2], in1=cnt_b[:, :],
                                     op0=ALU.mult, op1=ALU.add).then_inc(cnt_step, 1)
            dve.wait_ge(cnt_step, 4)
            dve.scalar_tensor_tensor(out=cnt[:, :], in0=is_ty[:, 2, :], scalar=float(S - 1), in1=cnt_a[:, :],
                                     op0=ALU.mult, op1=ALU.add).then_inc(cnt_ready, 1)
            dve.wait_ge(ex_in, 16)
            dve.tensor_copy(ex_f[:, :], ex_ids[:, :]).then_inc(ex_step, 1)
            dve.wait_ge(ex_step, 1)
            dve.tensor_scalar(ex_off[:, :], ex_f[:, :], float(R), prow[:, :], ALU.mult, ALU.subtract).then_inc(ex_step, 1)
            dve.wait_ge(ex_step, 2)
            dve.tensor_scalar(ex_le[:, :], ex_off[:, :], 0.0, ALPHA, ALU.is_le, ALU.mult).then_inc(ex_step, 1)
            dve.wait_ge(ex_step, 3)
            dve.scalar_tensor_tensor(out=ex_mask[:, :], in0=ex_off[:, :], scalar=float(1 - R), in1=ex_le[:, :],
                                     op0=ALU.is_ge, op1=ALU.mult).then_inc(ex_ready, 1)
            dve.wait_ge(w2_t_act, 1)
            dve.wait_ge(w2_t_dve, 1)
            select_w2(0)
            make_x1(1)
            dve.wait_ge(cb_turned, 1)
            dve.tensor_scalar(cb_t[:, 0:NC, :].rearrange("r c n -> r (c n)"), bank[4][0:R, :], ALPHA, None, ALU.mult)\
               .then_inc(cb_ready, 1)
            dve.wait_ge(mask_ready, 1)
            below_top(0)
            select_w2(1)
            block_probs(0)
            below_top(1)
            block_probs(1)
            prep_low(0, "wi", bank[6], NC * P)
            dve.wait_ge(cnt_ready, 1)
            make_x2(0)
            prep_low(1, "ewi_b", bank[7], NC * P)
            make_x2(1)
            dve.wait_ge(prep_turned, 3)
            dve.wait_ge(prep_hi, 3)
            dve.tensor_scalar(cb_t[:, NC, :], bank[4][0:R, 2 * P:3 * P], ALPHA, None, ALU.mult).then_inc(cb_ready, 1)
            prep_low(2, "small", bank[4], 2 * P)
            make_x3(0)
            prep_low(3, "ewo_a", bank[5], NC * P)
            make_x3(1)
            x3_low(0)
            x3_low(1)
            prep_low(4, "wo", bank[4], NC * P)
            dve.wait_ge(ex_ready, 1)
            mask_low(0, 0, RING[0], low_done, low_m)
            select_w2(2)
            low_low(0, 0, low_hi_ready, low_lo_ready)
            add_b0(2, bank[0])
            add_b0(3, bank[1])
            make_x1(2)
            hidden_lo(0, 0)
            make_x1(3)
            hidden_lo(0, 1)
            select_w2(3)
            hidden_lo(0, 2)
            hidden_lo(0, 3)
            below_top(2)
            below_top(3)
            block_probs(2)
            block_probs(3)
            make_x2(2)
            mask_low(1, 0, LOW2, low2_done, low2_m)
            make_x2(3)
            low_low(1, 0, low2_hi_ready, low2_lo_ready)
            make_x3(2)
            make_x3(3)
            x3_low(2)
            x3_low(3)
            finish(0)
            mask_low(0, 1, RING[2], low_done, low_m)
            low_low(0, 1, low_hi_ready, low_lo_ready)
            for c in range(NC):
                hidden_lo(1, c)
            mask_low(1, 1, LOW2, low2_done, low2_m)
            low_low(1, 1, low2_hi_ready, low2_lo_ready)
            finish(1)


_INS = ["x", "itok_B_0_63", "itok_B_0_2", "itok_B_0_7", "L0_cond_W", "L0_cond_b", "L1_cond_W1", "L1_cond_b1",
        "L1_cond_v", "L2_cond_weight", "L2_cond_bias", "L3_cond_wi", "L3_cond_wo", "L3_cond_common_wi_a",
        "L3_cond_common_wi_b", "L3_cond_common_wo_a", "L3_cond_common_wo_b", "L3_cond_experts_wi_a",
        "L3_cond_experts_wi_b", "L3_cond_experts_wo_a", "L3_cond_experts_wo_b"]


def kernel(**inputs):
    import numpy as _np
    import concourse.bacc as _bacc
    from concourse import mybir as _mybir
    from concourse.bass_utils import run_bass_kernel_spmd as _run

    nc = _bacc.Bacc("TRN2", target_bir_lowering=False, num_devices=1)
    arrays, args = {}, []
    for name in _INS:
        a = _np.ascontiguousarray(inputs[name])
        arrays[f"in_{name}_dram"] = a
        args.append(nc.dram_tensor(f"in_{name}_dram", a.shape, _mybir.dt.from_np(a.dtype), kind="ExternalInput").ap())
    shape = tuple(_np.shape(inputs["x"]))
    args.append(nc.dram_tensor("out_0_dram", shape, _mybir.dt.from_np(_np.dtype("float32")), kind="ExternalOutput").ap())
    build_program(nc, *args)
    r = _run(nc, [arrays], core_ids=[0])
    return r.results[0]["out_0_dram"]
```

```python
from contextlib import ExitStack

import concourse.bass as bass
from concourse import mybir

F32 = mybir.dt.float32
F32R = mybir.dt.float32r
I32 = mybir.dt.int32
BF16 = mybir.dt.bfloat16
ALU = mybir.AluOpType
ACT = mybir.ActivationFunctionType
AX_X = mybir.AxisListType.X

P = 128
ALPHA = 2.0
NEG_INF = -1e30


CONSTS = (("ident", P), ("quad", P), ("dist", 32), ("own", 32), ("krow", 1), ("prow", 1))


def build_program(nc, x, ids, consts, W0, bias, w1, W2_t, wi_side, wo_side, common, out):
    B, S, D = x.shape
    NCAT = W0.shape[0]
    A = w1.shape[1] - 2
    E = W2_t.shape[1]
    R = common.shape[0]
    F = common.shape[1] // 2 - D
    Q = P // S
    NT = B // Q
    NG = NT // 2
    GB = 2 * Q
    HT = NT // 2
    HB = B // 2
    HN = HT * P
    NC = F // P
    assert D == P and S == 32 and A == 32 and E * R == P and HN == 512 and NT == 8 and NC == 4
    KB = NCAT + E
    CAT, TYPE, EXPERT = (slice(n * B, n * B + B) for n in range(3))
    PG = 3
    SG = GB - PG

    with ExitStack() as ctx:
        def sb(name, shape, dt=F32):
            return ctx.enter_context(nc.sbuf_tensor(name, shape, dt))

        def sem(name):
            return ctx.enter_context(nc.semaphore(name))

        bank = [ctx.enter_context(nc.psum_tensor(f"bank{i}", [P, 512], F32)) for i in range(8)]
        MIX0 = [bank[2], bank[3], bank[7], bank[5]]
        MIX = [bank[2], bank[3], bank[3], bank[2]]
        MIX2 = [bank[2], bank[3], bank[3], bank[2]]
        TURN1 = [bank[0], bank[1], bank[0], bank[1]]
        TURN = [bank[0], bank[1], bank[0], bank[1]]
        LOW2, OUT = bank[3], bank[4]
        RING = [bank[6], bank[7], bank[5]]

        consts_sb = sb("consts_sb", [P, sum(n for _, n in CONSTS)])
        cols, at = {}, 0
        for name, n in CONSTS:
            cols[name] = consts_sb[:, at:at + n]
            at += n
        ident = cols["ident"]
        quad = cols["quad"].rearrange("p (q s) -> p q s", q=Q)
        dist, own = cols["dist"], cols["own"]
        krow, prow = cols["krow"], cols["prow"]
        ids_sb = sb("ids_sb", [P, 3 * B], I32)
        ids_f = sb("ids_f", [P, 3 * B])
        oh_idf = sb("oh_idf", [KB, B])
        onehot = sb("onehot", [KB, NT, Q, S])
        ty_own = sb("ty_own", [P, NT, Q])
        ty = sb("ty", [P, NT])
        is_ty = sb("is_ty", [P, 3, NT])
        hide_sign = sb("hide_sign", [P, NT])
        hide_side = sb("hide_side", [P, NT, S])
        hide_own = sb("hide_own", [P, NT, S])
        hidden = sb("hidden", [P, NT, S])
        n_hidden = sb("n_hidden", [P, NT])
        cnt = sb("cnt", [P, NT])
        ex_off = sb("ex_off", [P, B])
        ex_le = sb("ex_le", [P, B])
        ex_mask = sb("ex_mask", [P, B])
        warm = sb("warm", [1, 1])
        busy = sb("busy", [P, 512], BF16)
        bias_rows = sb("bias_rows", [KB, 2 * D])
        w0_sb = sb("w0_sb", [P, B, D])
        w1_sb = sb("w1_sb", [P, A + 2])
        v_blocks = sb("v_blocks", [P, Q, S])
        w2_t = sb("w2_t", [P, E, D])
        w2_sel = sb("w2_sel", [P, B, D])
        wi_side_sb = sb("wi_side_sb", [P, 2 * F + 2 * P])
        wo_side_sb = sb("wo_side_sb", [P, 2 * F])
        common_sb = sb("common_sb", [R, 2 * F + 2 * D])
        cwi_a, cwi_b = common_sb[:, 0:D], common_sb[:, D:D + F]
        cwo_a, cwo_b = common_sb[:, D + F:D + 2 * F], common_sb[:, D + 2 * F:]
        wi_sum = sb("wi_sum", [P, F])
        wo_sum = sb("wo_sum", [P, F])
        wide = {"wi": wi_sum[:, :], "ewi_b": wi_side_sb[:, F:2 * F], "small": wi_side_sb[:, 2 * F:],
                "wo": wo_sum[:, :], "ewo_a": wo_side_sb[:, F:2 * F]}
        split = {w: (sb(w + "_hi", [P, a.shape[1]], F32R), sb(w + "_lo", [P, a.shape[1]], F32R))
                 for w, a in wide.items()}
        x0 = sb("x0", [P, NT, D])
        x0_t = sb("x0_t", [P, NT, P])
        x1 = sb("x1", [P, NT, D + 2])
        x1_t = sb("x1_t", [P, NT, P])
        attn = sb("attn", [P, NT, S])
        scores = sb("scores", [P, NT, S])
        top = sb("top", [P, NT])
        below = sb("below", [P, NT, S])
        below_t = sb("below_t", [P, NT, S])
        probs_t = sb("probs_t", [P, NT, S])
        probs_b = sb("probs_b", [P, NT, Q, S])
        den = sb("den", [P, NT])
        rden = sb("rden", [P, NT])
        x2 = sb("x2", [P, NT, D])
        x2_t = sb("x2_t", [P, NT, P])
        x3 = sb("x3", [P, NT, D])
        x3_hi = sb("x3_hi", [P, NT * P], F32R)
        x3_lo = sb("x3_lo", [P, NT * P], F32R)
        low = [[sb(f"low{k}{h}", [P, HN]) for h in range(2)] for k in range(2)]
        low_hi = [[sb(f"low{k}_hi{h}", [P, HN], F32R) for h in range(2)] for k in range(2)]
        low_lo = [[sb(f"low{k}_lo{h}", [P, HN], F32R) for h in range(2)] for k in range(2)]
        hid_hi = [sb(f"hid_hi{c}", [P, HN], F32R) for c in range(NC)]
        hid_lo = [sb(f"hid_lo{c}", [P, HN], F32R) for c in range(NC)]
        mlp_t = [sb(f"mlp_t{h}", [P, HN]) for h in range(2)]
        out_sb = sb("out_sb", [P, NT, D])

        x_in = [sem(f"x_in{h}") for h in range(2)]
        w0_in = [sem(f"w0_in{g}") for g in range(NG)]
        w0_in_pool = [sem(f"w0_in_pool{g}") for g in range(NG)]
        ids_in, consts_in, w1_in, w2_in, bias_in, wi_in, wo_in, common_in = (sem(n) for n in (
            "ids_in", "consts_in", "w1_in", "w2_in", "bias_in", "wi_in", "wo_in", "common_in"))
        out_done = sem("out_done")
        w2_sel_pool = sem("w2_sel_pool")
        x0_turned, x1_turned, x2_turned, x3_turned = (sem(f"x{k}_turned") for k in range(4))
        wi_common, wo_common = sem("wi_common"), sem("wo_common")
        l0_done, attn_in, scores_done, pooled, l2_done = (sem(n) for n in (
            "l0_done", "attn_in", "scores_done", "pooled", "l2_done"))
        low_done, hid_done, low2_done, mlp_done, mlp_turned = (sem(n) for n in (
            "low_done", "hid_done", "low2_done", "mlp_done", "mlp_turned"))
        x0_t_ready, x1_t_ready, x2_t_ready, x3_hi_ready = (sem(n) for n in (
            "x0_t_ready", "x1_t_ready", "x2_t_ready", "x3_hi_ready"))
        warm_done, w2_sel_act, x0_t_ready_act, attn_ready, exp_ready = (sem(n) for n in (
            "warm_done", "w2_sel_act", "x0_t_ready_act", "attn_ready", "exp_ready"))
        hi_ready = {w: sem(w + "_hi_ready") for w in wide}
        low_hi_ready, hid_hi_ready, low2_hi_ready, mlp_copied = (sem(n) for n in (
            "low_hi_ready", "hid_hi_ready", "low2_hi_ready", "mlp_copied"))
        idf_ready, onehot_ready, ex_step, ex_ready, ty_step, mask_step, ones_ready = (
            sem(n) for n in ("idf_ready", "onehot_ready", "ex_step", "ex_ready", "ty_step", "mask_step",
                             "ones_ready"))
        mask_ready, cnt_step, cnt_ready, v_ready, wi_summed, wo_summed = (sem(n) for n in (
            "mask_ready", "cnt_step", "cnt_ready", "v_ready", "wi_summed", "wo_summed"))
        lo_ready = {w: sem(w + "_lo_ready") for w in wide}
        busy_ready, x1_ready, masked, top_ready, below_ready, below_t_ready = (sem(n) for n in (
            "busy_ready", "x1_ready", "masked", "top_ready", "below_ready", "below_t_ready"))
        probs_ready, den_ready, rden_ready, x2_ready, x3_ready, x3_lo_ready = (sem(n) for n in (
            "probs_ready", "den_ready", "rden_ready", "x2_ready", "x3_ready", "x3_lo_ready"))
        hid_used = sem("hid_used")
        low_m, low_lo_ready, hid_lo_ready, low2_m, low2_lo_ready, out_ready = (sem(n) for n in (
            "low_m", "low_lo_ready", "hid_lo_ready", "low2_m", "low2_lo_ready", "out_ready"))

        def tiles(g):
            return slice(2 * g, 2 * g + 2)

        def group_bank(b, w=P):
            return b[:, 0:2 * w].rearrange("p (t n) -> p t n", t=2)

        x_tok = x.rearrange("b s d -> (b s) d").rearrange("(t p) d -> p t d", p=P)
        out_tok = out.rearrange("b s d -> (b s) d").rearrange("(t p) d -> p t d", p=P)
        def gather_w0(eng, regs, b_first, landed):
            for k, reg in enumerate(regs):
                cat = eng.snap(reg, min_val=0, max_val=NCAT - 1)
                eng.dma_start(w0_sb[:, b_first + k, :], W0[bass.ds(cat, 1), :, :].rearrange("o d h -> (o d) h"))\
                   .then_inc(landed, 16)

        block = ctx.enter_context(nc.Block())

        @block.sync
        def _(sp):
            regs = [[sp.alloc_register(f"sp_cat{g}_{k}") for k in range(SG)] for g in range(2)]
            sp.load(regs[0], ids[0:1, 0:SG])
            gather_w0(sp, regs[0], 0, w0_in[0])
            sp.dma_start(w1_sb[:, :], w1).then_inc(w1_in, 16)
            for g in range(1, NG):
                sp.wait_ge(ids_in, 16)
                sp.load(regs[g % 2], ids_sb[0:1, GB * g:GB * g + SG])
                gather_w0(sp, regs[g % 2], GB * g, w0_in[g])
                if g == 1:
                    sp.dma_start(common_sb[:, :], common).then_inc(common_in, 16)
                    sp.dma_start(w2_t[:, :, :], W2_t).then_inc(w2_in, 16)
                    sp.dma_start(x0[:, HT:NT, :], x_tok[:, HT:NT, :]).then_inc(x_in[1], 16)
                    sp.dma_start(wi_side_sb[:, :], wi_side).then_inc(wi_in, 16)
            sp.dma_start(wo_side_sb[:, :], wo_side).then_inc(wo_in, 16)
            for h in range(2):
                for k in range(2):
                    g = 2 * h + k
                    sp.wait_ge(out_ready, g + 1)
                    sp.dma_start(out_tok[:, tiles(g), :], out_sb[:, tiles(g), :]).then_inc(out_done, 16)
            sp.wait_ge(out_done, 16 * NG)

        @block.gpsimd
        def _(pool):
            regs = [[pool.alloc_register(f"pool_cat{g}_{k}") for k in range(PG)] for g in range(2)]
            pool.load(regs[0], ids[0:1, SG:GB])
            gather_w0(pool, regs[0], SG, w0_in_pool[0])
            pool.wait_ge(ids_in, 16)
            for g in range(1, NG):
                pool.load(regs[g % 2], ids_sb[0:1, GB * g + SG:GB * g + GB])
                gather_w0(pool, regs[g % 2], GB * g + SG, w0_in_pool[g])
            ex_regs = [[pool.alloc_register(f"pool_ex{g}_{k}") for k in range(GB)] for g in range(2)]

            def select_w2(g):
                pool.load(ex_regs[g % 2], ids_sb[0:1, 2 * B + GB * g:2 * B + GB * g + GB])
                for k, reg in enumerate(ex_regs[g % 2], GB * g):
                    e = pool.snap(reg, min_val=0, max_val=E - 1)
                    pool.tensor_copy(w2_sel[:, k, :], w2_t[:, bass.ds(e, 1), :].rearrange("p o n -> p (o n)"))\
                        .then_inc(w2_sel_pool, 1)

            def weight_low(w):
                pool.wait_ge(hi_ready[w], 1)
                pool.tensor_tensor(split[w][1][:, :], wide[w], split[w][0][:, :].bitcast(F32), ALU.subtract)\
                    .then_inc(lo_ready[w], 1)

            pool.wait_ge(w2_in, 16)
            select_w2(1)
            weight_low("wi")
            weight_low("ewi_b")
            select_w2(2)
            weight_low("ewo_a")
            select_w2(3)
            weight_low("wo")

        @block.tensor
        def _(pe):
            def turn_x(src, g, b, done):
                for k in range(2):
                    mm = pe.transpose(b[:, k * P:k * P + P], src[:, 2 * g + k, 0:D], ident)
                mm.then_inc(done, 1)

            def keep_busy(n, b):
                for _ in range(n):
                    pe.matmul(b[:, :], busy[:, 0:P], busy[:, :], start=True, stop=True, skip_group_check=True)

            def turn_x0(h):
                pe.wait_ge(x_in[h], 16)
                for k in range(HT):
                    mm = pe.transpose(bank[5][:, k * P:k * P + P], x0[:, HT * h + k, :], ident)
                mm.then_inc(x0_turned, 1)

            def add_bias(g, b, k):
                for t in range(2):
                    pe.matmul(b[:, t * D:t * D + D], onehot[:, 2 * g + t, :, :].rearrange("k q s -> k (q s)"),
                              bias_rows[:, k * D:k * D + D], start=t == 0, stop=False, skip_group_check=True)

            def rows_times(src_t, w, b, g, done):
                for k in range(2):
                    for q in range(Q):
                        t = 2 * g + k
                        mm = pe.matmul(b[q * S:q * S + S, k * D:k * D + D], src_t[:, t, q * S:q * S + S],
                                       w[:, Q * t + q, :], start=False, stop=True, skip_group_check=True)
                mm.then_inc(done, 1)

            def layer0(g):
                pe.wait_ge(w0_in[g], 16 * SG)
                pe.wait_ge(w0_in_pool[g], 16 * PG)
                pe.wait_ge((x0_t_ready, x0_t_ready_act)[g // 2], 1)
                rows_times(x0_t, w0_sb, MIX0[g], g, l0_done)

            def turn_x1(g):
                pe.wait_ge(x1_ready, g + 1)
                turn_x(x1, g, TURN1[g], x1_turned)

            def attn_product(g):
                pe.wait_ge(x1_t_ready, g + 1)
                for q in range(Q):
                    mm = pe.matmul(MIX[g][q * S:q * S + S, 0:2 * S].rearrange("p (t l) -> p t l", t=2),
                                   w1_sb[:, 0:A], x1_t[:, tiles(g), q * S:q * S + S], start=True, stop=True)
                mm.then_inc(attn_in, 1)

            def score_product(g):
                pe.wait_ge(attn_ready, g + 1)
                pe.wait_ge(v_ready, 1)
                for q in range(Q):
                    mm = pe.matmul(MIX[g][q * S:q * S + S, 0:2 * S].rearrange("p (t l) -> p t l", t=2),
                                   v_blocks[:, q, :], attn[:, tiles(g), :], start=True, stop=True)
                mm.then_inc(scores_done, 1)

            def pool_rows(g):
                pe.wait_ge(probs_ready, g + 1)
                pe.wait_ge(ones_ready, 1)
                for k in range(2):
                    mm = pe.matmul(MIX[g][:, 256 * k:256 * k + D + 1],
                                   probs_b[:, 2 * g + k, :, :].rearrange("p q j -> p (q j)"),
                                   x1[:, 2 * g + k, 0:D + 1], start=True, stop=True)
                mm.then_inc(pooled, 1)

            def turn_x2(g):
                pe.wait_ge(x2_ready, 2 * (g + 1))
                turn_x(x2, g, TURN[g], x2_turned)

            def layer2(g):
                pe.wait_ge(x2_t_ready, g + 1)
                if g == 0:
                    pe.wait_ge(w2_sel_act, GB)
                else:
                    pe.wait_ge(w2_sel_pool, GB * g)
                rows_times(x2_t, w2_sel, MIX2[g], g, l2_done)

            def turn_x3(g):
                pe.wait_ge(x3_ready, g + 1)
                turn_x(x3, g, TURN[g], x3_turned)

            def three(acc, w, col, hi, lo, first, last):
                w_hi, w_lo = split[w]
                c = slice(col * P, col * P + P)
                pe.matmul(acc, w_hi[:, c], hi, start=first, stop=False, skip_group_check=True)
                pe.matmul(acc, w_hi[:, c], lo, start=False, stop=False, skip_group_check=True)
                return pe.matmul(acc, w_lo[:, c], hi, start=False, stop=last, skip_group_check=True)

            def ring(h, k):
                return RING[(5 * h + k) % 3][:, :]

            def half(a, h):
                return a[:, HN * h:HN * h + HN]

            def wait_ring(h, k):
                n = 5 * h + k - 3
                if n in (0, 5):
                    pe.wait_ge(low_m, n // 5 + 1)
                elif n > 0:
                    pe.wait_ge(hid_lo_ready, n - n // 5)

            def low_rank(h):
                wait_ring(h, 0)
                pe.wait_ge(x3_hi_ready, 2 * (h + 1))
                pe.wait_ge(x3_lo_ready, 2 * (h + 1))
                three(ring(h, 0), "small", 0, half(x3_hi, h), half(x3_lo, h), True, True).then_inc(low_done, 1)

            def hidden_dense(h, c):
                wait_ring(h, c + 1)
                three(ring(h, c + 1), "wi", c, half(x3_hi, h), half(x3_lo, h), True, False)

            def hidden_low(h, c):
                if c == 0:
                    pe.wait_ge(low_hi_ready, h + 1)
                    pe.wait_ge(low_lo_ready, h + 1)
                three(ring(h, c + 1), "ewi_b", c, low_hi[0][h][:, :], low_lo[0][h][:, :], False, True)\
                    .then_inc(hid_done, 1)

            def out_low(h, c):
                pe.wait_ge(hid_hi_ready, 4 * h + c + 1)
                pe.wait_ge(hid_lo_ready, 4 * h + c + 1)
                if c == 0 and h == 1:
                    pe.wait_ge(low2_m, 1)
                mm = three(LOW2[:, :], "ewo_a", c, hid_hi[c][:, :], hid_lo[c][:, :], c == 0, c == NC - 1)
                if c == NC - 1:
                    mm.then_inc(low2_done, 1)

            def out_dense(h, c):
                if c == 0 and h == 1:
                    pe.wait_ge(mlp_copied, 2)
                mm = three(OUT[:, :], "wo", c, hid_hi[c][:, :], hid_lo[c][:, :], c == 0, False)
                mm.then_inc(hid_used, 1)

            def out_expert(h):
                pe.wait_ge(low2_hi_ready, 1 + 2 * h)
                pe.wait_ge(low2_lo_ready, 1 + 2 * h)
                three(OUT[:, :], "small", 1, low_hi[1][h][:, :], low_lo[1][h][:, :], False, True)\
                    .then_inc(mlp_done, 1)

            def turn_mlp(h):
                pe.wait_ge(x3_lo_ready, NG)
                for g in (2 * h, 2 * h + 1):
                    pe.wait_ge(mlp_copied, g + 1)
                    if h == 1:
                        pe.wait_ge(out_ready, g - 1)
                    for k in range(2):
                        t = 2 * (g % 2) + k
                        mm = pe.transpose(TURN[g][:, k * P:k * P + P], mlp_t[h][:, t * P:t * P + P], ident)
                    mm.then_inc(mlp_turned, 1)

            def common_wi(c):
                mm = pe.matmul(bank[6][:, c * P:c * P + P], cwi_a, cwi_b[:, c * P:c * P + P], start=True, stop=True)
                if c == NC - 1:
                    mm.then_inc(wi_common, 1)

            def common_wo(c):
                mm = pe.matmul(bank[4][:, c * P:c * P + P], cwo_a[:, c * P:c * P + P], cwo_b, start=True, stop=True)
                if c == NC - 1:
                    mm.then_inc(wo_common, 1)

            pe.wait_ge(busy_ready, 1)
            keep_busy(8, bank[0])
            pe.wait_ge(consts_in, 16)
            turn_x0(0)
            pe.wait_ge(onehot_ready, 1)
            pe.wait_ge(bias_in, 16)
            add_bias(0, MIX0[0], 0)
            add_bias(1, MIX0[1], 0)
            keep_busy(3, bank[0])
            layer0(0)
            keep_busy(2, bank[1])
            turn_x1(0)
            keep_busy(1, bank[1])
            pe.wait_ge(w1_in, 16)
            attn_product(0)
            keep_busy(2, bank[1])
            layer0(1)
            score_product(0)
            keep_busy(1, bank[0])
            turn_x1(1)
            pe.wait_ge(common_in, 16)
            common_wi(0)
            common_wi(1)
            attn_product(1)
            keep_busy(2, bank[0])
            score_product(1)
            pool_rows(0)
            common_wi(2)
            common_wi(3)
            pe.wait_ge(onehot_ready, 2)
            add_bias(2, MIX0[2], 0)
            turn_x0(1)
            for c in range(NC):
                common_wo(c)
            pool_rows(1)
            turn_x2(0)
            pe.wait_ge(x0_t_ready_act, 1)
            add_bias(3, MIX0[3], 0)
            pe.wait_ge(x2_ready, 2)
            add_bias(0, MIX2[0], 1)
            layer2(0)
            turn_x2(1)
            add_bias(1, MIX2[1], 1)
            turn_x3(0)
            layer2(1)
            layer0(2)
            turn_x3(1)
            layer0(3)
            pe.wait_ge(x3_lo_ready, 1)
            turn_x1(2)
            pe.wait_ge(hi_ready["small"], 1)
            pe.wait_ge(lo_ready["small"], 1)
            low_rank(0)
            pe.wait_ge(x3_ready, 2)
            attn_product(2)
            pe.wait_ge(hi_ready["wi"], 1)
            pe.wait_ge(lo_ready["wi"], 1)
            hidden_dense(0, 0)
            score_product(2)
            pe.wait_ge(x1_ready, 4)
            hidden_dense(0, 1)
            pe.wait_ge(x3_lo_ready, 2)
            turn_x1(3)
            hidden_dense(0, 2)
            attn_product(3)
            pe.wait_ge(hi_ready["ewi_b"], 1)
            pe.wait_ge(lo_ready["ewi_b"], 1)
            hidden_low(0, 0)
            pool_rows(2)
            hidden_low(0, 1)
            score_product(3)
            hidden_low(0, 2)
            turn_x2(2)
            hidden_dense(0, 3)
            add_bias(2, MIX2[2], 1)
            layer2(2)
            hidden_low(0, 3)
            turn_x3(2)
            pe.wait_ge(x3_ready, 3)
            pe.wait_ge(hi_ready["ewo_a"], 1)
            pe.wait_ge(lo_ready["ewo_a"], 1)
            out_low(0, 0)
            pool_rows(3)
            out_low(0, 1)
            out_low(0, 2)
            out_low(0, 3)
            turn_x2(3)
            add_bias(3, MIX2[3], 1)
            pe.wait_ge(hi_ready["wo"], 1)
            pe.wait_ge(lo_ready["wo"], 1)
            out_dense(0, 0)
            layer2(3)
            out_dense(0, 1)
            turn_x3(3)
            out_dense(0, 2)
            out_dense(0, 3)
            low_rank(1)
            out_expert(0)
            for c in range(3):
                hidden_dense(1, c)
            for c in range(3):
                hidden_low(1, c)
            turn_mlp(0)
            out_low(1, 0)
            hidden_dense(1, 3)
            hidden_low(1, 3)
            out_low(1, 1)
            out_low(1, 2)
            out_dense(1, 0)
            out_low(1, 3)
            for c in range(1, NC):
                out_dense(1, c)
            out_expert(1)
            turn_mlp(1)

        @block.scalar
        def _(act):
            regs = [act.alloc_register(f"act_ex{k}") for k in range(GB)]

            def copy_turned(dst, b, g, col, turned, ready):
                act.wait_ge(turned, g + 1)
                act.copy(dst[:, tiles(g), :].rearrange("p t n -> p (t n)"), b[:, col:col + 2 * P]).then_inc(ready, 1)

            def select_w2(g):
                for k in range(GB):
                    e = act.snap(regs[GB * g + k], min_val=0, max_val=E - 1)
                    act.copy(w2_sel[:, GB * g + k, :], w2_t[:, bass.ds(e, 1), :].rearrange("p o n -> p (o n)"))\
                       .then_inc(w2_sel_act, 1)

            def copy_x0():
                act.wait_ge(x0_turned, 2)
                act.copy(x0_t[:, HT:NT, :].rearrange("p t n -> p (t n)"), bank[5][:, :]).then_inc(x0_t_ready_act, 1)

            def attn_tanh(g):
                act.wait_ge(attn_in, g + 1)
                act.activation(attn[:, tiles(g), :].rearrange("p t l -> p (t l)"), MIX[g][:, 0:2 * S], ACT.Tanh,
                               bias=w1_sb[:, A:A + 1]).then_inc(attn_ready, 1)

            def exp_scores(g):
                act.wait_ge(below_t_ready, g + 1)
                act.activation(probs_t[:, tiles(g), :].rearrange("p t l -> p (t l)"),
                               below_t[:, tiles(g), :].rearrange("p t l -> p (t l)"), ACT.Exp).then_inc(exp_ready, 1)

            def x3_high(g):
                act.wait_ge(x3_turned, g + 1)
                act.copy(x3_hi[:, 2 * P * g:2 * P * (g + 1)], TURN[g][:, 0:2 * P]).then_inc(x3_hi_ready, 1)

            def weight_high(w):
                act.copy(split[w][0][:, :], wide[w]).then_inc(hi_ready[w], 1)

            def low_high(k, h, m, ready, parts=1):
                for i in range(parts):
                    act.wait_ge(m, h + 1 + i)
                    c = slice(i * HN // parts, (i + 1) * HN // parts)
                    act.copy(low_hi[k][h][:, c], low[k][h][:, c]).then_inc(ready, 1)

            def hidden_high(h, c):
                act.wait_ge(hid_done, 4 * h + c + 1)
                if h == 1:
                    act.wait_ge(hid_used, c + 1)
                act.activation(hid_hi[c][:, :], RING[(5 * h + c + 1) % 3][:, :], ACT.Relu).then_inc(hid_hi_ready, 1)

            def copy_mlp(h):
                act.wait_ge(mlp_done, h + 1)
                for k in range(2):
                    c = slice(2 * P * k, 2 * P * (k + 1))
                    act.copy(mlp_t[h][:, c], OUT[:, c]).then_inc(mlp_copied, 1)

            act.dma_start(ids_sb[:, :], ids.partition_broadcast(P)).then_inc(ids_in, 16)
            act.dma_start(consts_sb[:, :], consts).then_inc(consts_in, 16)
            act.dma_start(x0[:, 0:HT, :], x_tok[:, 0:HT, :]).then_inc(x_in[0], 16)
            act.dma_start(bias_rows[:, :], bias).then_inc(bias_in, 16)
            act.wait_ge(ones_ready, 1)
            act.activation(warm[:, :], x1[0:1, 0, D:D + 1], ACT.Exp).then_inc(warm_done, 1)
            act.wait_ge(ids_in, 16)
            act.load(regs, ids_sb[0:1, 2 * B:2 * B + GB])
            copy_turned(x1_t, TURN1[0], 0, 0, x1_turned, x1_t_ready)
            attn_tanh(0)
            copy_turned(x1_t, TURN1[1], 1, 0, x1_turned, x1_t_ready)
            exp_scores(0)
            attn_tanh(1)
            act.wait_ge(w2_in, 16)
            select_w2(0)
            exp_scores(1)
            copy_x0()
            copy_turned(x2_t, TURN[0], 0, 0, x2_turned, x2_t_ready)
            act.wait_ge(wi_in, 16)
            weight_high("small")
            copy_turned(x2_t, TURN[1], 1, 0, x2_turned, x2_t_ready)
            act.wait_ge(wi_summed, 1)
            weight_high("wi")
            x3_high(0)
            weight_high("ewi_b")
            x3_high(1)
            copy_turned(x1_t, TURN1[2], 2, 0, x1_turned, x1_t_ready)
            act.wait_ge(wo_in, 16)
            weight_high("ewo_a")
            attn_tanh(2)
            low_high(0, 0, low_m, low_hi_ready)
            copy_turned(x1_t, TURN1[3], 3, 0, x1_turned, x1_t_ready)
            exp_scores(2)
            act.wait_ge(wo_summed, 1)
            weight_high("wo")
            attn_tanh(3)
            hidden_high(0, 0)
            hidden_high(0, 1)
            copy_turned(x2_t, TURN[2], 2, 0, x2_turned, x2_t_ready)
            exp_scores(3)
            hidden_high(0, 2)
            x3_high(2)
            hidden_high(0, 3)
            copy_turned(x2_t, TURN[3], 3, 0, x2_turned, x2_t_ready)
            x3_high(3)
            low_high(1, 0, low2_m, low2_hi_ready)
            low_high(0, 1, low_m, low_hi_ready)
            copy_mlp(0)
            for c in range(NC):
                hidden_high(1, c)
            low_high(1, 1, low2_m, low2_hi_ready, parts=2)
            copy_mlp(1)

        @block.vector
        def _(dve):
            def copy_x0():
                dve.wait_ge(x0_turned, 1)
                dve.tensor_copy(x0_t[:, 0:HT, :].rearrange("p t n -> p (t n)"), bank[5][:, :]).then_inc(x0_t_ready, 1)

            def make_x1(g):
                dve.wait_ge(l0_done, g + 1)
                dve.wait_ge(x_in[g // 2], 16)
                dve.tensor_tensor(x1[:, tiles(g), 0:D], group_bank(MIX0[g]), x0[:, tiles(g), :], ALU.add)\
                   .then_inc(x1_ready, 1)

            def below_top(g):
                t = tiles(g)
                dve.wait_ge(scores_done, g + 1)
                dve.scalar_tensor_tensor(out=scores[:, t, :], in0=hidden[:, t, :], scalar=NEG_INF,
                                         in1=group_bank(MIX[g], S), op0=ALU.mult, op1=ALU.add).then_inc(masked, 1)
                dve.wait_ge(masked, g + 1)
                dve.tensor_reduce(top[:, t], scores[:, t, :], AX_X, ALU.max).then_inc(top_ready, 1)
                dve.wait_ge(top_ready, g + 1)
                dve.tensor_tensor(below[:, t, :], scores[:, t, :], top[:, t].unsqueeze(2).to_broadcast([P, 2, S]),
                                  ALU.subtract).then_inc(below_ready, 1)
                dve.wait_ge(below_ready, g + 1)
                dve.transpose(below_t[:, t, :].rearrange("p t l -> p (t l)"),
                              below[:, t, :].rearrange("p t l -> p (t l)")).then_inc(below_t_ready, 1)

            def block_probs(g):
                dve.wait_ge(exp_ready, g + 1)
                for k in range(2):
                    ins = dve.tensor_tensor(probs_b[:, 2 * g + k, :, :],
                                            probs_t[:, 2 * g + k, :].unsqueeze(1).to_broadcast([P, Q, S]),
                                            quad[:, :, :], ALU.mult)
                ins.then_inc(probs_ready, 1)

            def make_den(g):
                t = tiles(g)
                dve.wait_ge(pooled, g + 1)
                dve.tensor_tensor(den[:, t], MIX[g][:, :].rearrange("p (t n) -> p t n", t=2)[:, :, D],
                                  cnt[:, t], ALU.mult).then_inc(den_ready, 1)
                dve.wait_ge(den_ready, g + 1)
                dve.reciprocal(rden[:, t], den[:, t]).then_inc(rden_ready, 1)

            def make_x2(g):
                dve.wait_ge(rden_ready, g + 1)
                for k in range(2):
                    dve.scalar_tensor_tensor(out=x2[:, 2 * g + k, :], in0=MIX[g][:, 256 * k:256 * k + D],
                                             scalar=rden[:, 2 * g + k:2 * g + k + 1], in1=x1[:, 2 * g + k, 0:D],
                                             op0=ALU.mult, op1=ALU.add).then_inc(x2_ready, 1)

            def make_x3(g):
                dve.wait_ge(l2_done, g + 1)
                dve.tensor_tensor(x3[:, tiles(g), :], group_bank(MIX2[g]), x2[:, tiles(g), :], ALU.add)\
                   .then_inc(x3_ready, 1)

            def x3_low(g):
                c = slice(2 * P * g, 2 * P * (g + 1))
                dve.wait_ge(x3_hi_ready, g + 1)
                dve.tensor_tensor(x3_lo[:, c], TURN[g][:, 0:2 * P], x3_hi[:, c].bitcast(F32), ALU.subtract)\
                   .then_inc(x3_lo_ready, 1)

            def add_common(w_sum, w_t, b, done, ready):
                dve.wait_ge(done, 1)
                dve.scalar_tensor_tensor(out=w_sum[:, :], in0=b[:, :], scalar=ALPHA, in1=w_t[:, 0:F],
                                         op0=ALU.mult, op1=ALU.add).then_inc(ready, 1)

            def weight_low(w):
                dve.wait_ge(hi_ready[w], 1)
                dve.tensor_tensor(split[w][1][:, :], wide[w], split[w][0][:, :].bitcast(F32), ALU.subtract)\
                   .then_inc(lo_ready[w], 1)

            def mask_low(k, h, b, done, m, parts=1):
                dve.wait_ge(done, h + 1)
                n = HB // parts
                for i in range(parts):
                    c = slice(i * n * S, (i + 1) * n * S)
                    dve.tensor_tensor(low[k][h][:, c].rearrange("p (b s) -> p b s", s=S),
                                      b[:, c].rearrange("p (b s) -> p b s", s=S),
                                      ex_mask[:, HB * h + i * n:HB * h + i * n + n].unsqueeze(2).to_broadcast([P, n, S]),
                                      ALU.mult).then_inc(m, 1)

            def low_low(k, h, hi_ready, ready, parts=1):
                for i in range(parts):
                    dve.wait_ge(hi_ready, h + 1 + i)
                    c = slice(i * HN // parts, (i + 1) * HN // parts)
                    dve.tensor_tensor(low_lo[k][h][:, c], low[k][h][:, c], low_hi[k][h][:, c].bitcast(F32),
                                      ALU.subtract).then_inc(ready, 1)

            def hidden_lo(h, c):
                dve.wait_ge(hid_hi_ready, 4 * h + c + 1)
                dve.scalar_tensor_tensor(out=hid_lo[c][:, :], in0=RING[(5 * h + c + 1) % 3][:, :], scalar=0.0,
                                         in1=hid_hi[c][:, :].bitcast(F32), op0=ALU.max, op1=ALU.subtract)\
                   .then_inc(hid_lo_ready, 1)

            def finish(h):
                for g in (2 * h, 2 * h + 1):
                    dve.wait_ge(mlp_turned, g + 1)
                    dve.tensor_tensor(out_sb[:, tiles(g), :], group_bank(TURN[g]), x3[:, tiles(g), :],
                                      ALU.add).then_inc(out_ready, 1)

            dve.memset(busy[:, :], 0.0).then_inc(busy_ready, 1)
            dve.memset(x1[:, :, D:D + 2], 1.0).then_inc(ones_ready, 1)
            dve.wait_ge(ids_in, 16)
            dve.tensor_copy(oh_idf[0:NCAT, :], ids_sb[0:NCAT, CAT]).then_inc(idf_ready, 1)
            dve.tensor_copy(oh_idf[NCAT:KB, :], ids_sb[NCAT:KB, EXPERT]).then_inc(idf_ready, 1)
            dve.tensor_copy(ids_f[:, :], ids_sb[:, :]).then_inc(idf_ready, 1)
            dve.wait_ge(consts_in, 16)
            dve.wait_ge(idf_ready, 2)
            for h in range(2):
                dve.tensor_scalar(onehot[:, HT * h:HT * h + HT, :, :].rearrange("p t q s -> p (t q) s"),
                                  oh_idf[:, HB * h:HB * h + HB].unsqueeze(2).to_broadcast([KB, HB, S]),
                                  krow[0:KB, :], None, ALU.is_equal).then_inc(onehot_ready, 1)
            dve.wait_ge(idf_ready, 3)
            dve.tensor_tensor(ty_own[:, :, :], ids_f[:, TYPE].rearrange("p (t q) -> p t q", q=Q),
                              quad[:, :, 0].unsqueeze(1).to_broadcast([P, NT, Q]), ALU.mult).then_inc(ty_step, 1)
            copy_x0()
            dve.wait_ge(ty_step, 1)
            dve.tensor_reduce(ty[:, :], ty_own[:, :, :], AX_X, ALU.add).then_inc(ty_step, 1)
            dve.wait_ge(ty_step, 2)
            for n, op in enumerate((ALU.is_equal, ALU.is_equal, ALU.is_ge)):
                dve.tensor_scalar(is_ty[:, n, :], ty[:, :], float(n), None, op).then_inc(ty_step, 1)
            dve.wait_ge(ty_step, 5)
            dve.tensor_tensor(hide_sign[:, :], is_ty[:, 0, :], is_ty[:, 1, :], ALU.subtract).then_inc(mask_step, 1)
            dve.wait_ge(mask_step, 1)
            dve.tensor_tensor(hide_side[:, :, :], hide_sign[:, :].unsqueeze(2).to_broadcast([P, NT, S]),
                              dist.unsqueeze(1).to_broadcast([P, NT, S]), ALU.mult).then_inc(mask_step, 1)
            dve.tensor_tensor(hide_own[:, :, :], is_ty[:, 2, :].unsqueeze(2).to_broadcast([P, NT, S]),
                              own.unsqueeze(1).to_broadcast([P, NT, S]), ALU.mult).then_inc(mask_step, 1)
            dve.wait_ge(mask_step, 3)
            dve.scalar_tensor_tensor(out=hidden[:, :, :], in0=hide_side[:, :, :], scalar=0.0, in1=hide_own[:, :, :],
                                     op0=ALU.is_gt, op1=ALU.add).then_inc(mask_ready, 1)
            make_x1(0)
            dve.wait_ge(w1_in, 16)
            dve.tensor_scalar(v_blocks[:, :, :], quad, w1_sb[:, A + 1:A + 2], None, ALU.mult).then_inc(v_ready, 1)
            dve.wait_ge(mask_ready, 1)
            dve.tensor_reduce(n_hidden[:, :], hidden[:, :, :], AX_X, ALU.add).then_inc(cnt_step, 1)
            dve.wait_ge(cnt_step, 1)
            dve.tensor_scalar(cnt[:, :], n_hidden[:, :], -1.0, float(S), ALU.mult, ALU.add).then_inc(cnt_ready, 1)
            make_x1(1)
            below_top(0)
            block_probs(0)
            below_top(1)
            dve.wait_ge(cnt_ready, 1)
            make_den(0)
            block_probs(1)
            make_x2(0)
            make_den(1)
            make_x2(1)
            dve.wait_ge(wi_in, 16)
            add_common(wi_sum, wi_side_sb, bank[6], wi_common, wi_summed)
            make_x3(0)
            weight_low("small")
            dve.tensor_scalar(ex_off[:, :], ids_f[:, EXPERT], float(R), prow, ALU.mult, ALU.subtract).then_inc(ex_step, 1)
            make_x3(1)
            x3_low(0)
            make_x1(2)
            dve.wait_ge(ex_step, 1)
            dve.tensor_scalar(ex_le[:, :], ex_off[:, :], 0.0, ALPHA, ALU.is_le, ALU.mult).then_inc(ex_step, 1)
            x3_low(1)
            make_x1(3)
            dve.wait_ge(ex_step, 2)
            dve.scalar_tensor_tensor(out=ex_mask[:, :], in0=ex_off[:, :], scalar=float(1 - R), in1=ex_le[:, :],
                                     op0=ALU.is_ge, op1=ALU.mult).then_inc(ex_ready, 1)
            dve.wait_ge(ex_ready, 1)
            mask_low(0, 0, RING[0], low_done, low_m)
            below_top(2)
            low_low(0, 0, low_hi_ready, low_lo_ready)
            block_probs(2)
            dve.wait_ge(wo_in, 16)
            add_common(wo_sum, wo_side_sb, bank[4], wo_common, wo_summed)
            make_den(2)
            make_x2(2)
            hidden_lo(0, 0)
            below_top(3)
            hidden_lo(0, 1)
            block_probs(3)
            make_x3(2)
            hidden_lo(0, 2)
            x3_low(2)
            hidden_lo(0, 3)
            make_den(3)
            make_x2(3)
            make_x3(3)
            mask_low(1, 0, LOW2, low2_done, low2_m)
            x3_low(3)
            low_low(1, 0, low2_hi_ready, low2_lo_ready)
            mask_low(0, 1, RING[2], low_done, low_m)
            low_low(0, 1, low_hi_ready, low_lo_ready)
            for c in range(3):
                hidden_lo(1, c)
            finish(0)
            hidden_lo(1, 3)
            mask_low(1, 1, LOW2, low2_done, low2_m, parts=2)
            low_low(1, 1, low2_hi_ready, low2_lo_ready, parts=2)
            finish(1)


def kernel(x, itok_B_0_63, itok_B_0_2, itok_B_0_7, L0_cond_W, L0_cond_b, L1_cond_W1, L1_cond_b1, L1_cond_v,
           L2_cond_weight, L2_cond_bias, L3_cond_wi, L3_cond_wo, L3_cond_common_wi_a, L3_cond_common_wi_b,
           L3_cond_common_wo_a, L3_cond_common_wo_b, L3_cond_experts_wi_a, L3_cond_experts_wi_b,
           L3_cond_experts_wo_a, L3_cond_experts_wo_b):
    import numpy as _np
    import concourse.bacc as _bacc
    from concourse import mybir as _mybir
    from concourse.bass_utils import run_bass_kernel_spmd as _run

    S = x.shape[1]
    ncat, D = L0_cond_b.shape
    E = L2_cond_bias.shape[0]
    F = L3_cond_wi.shape[0]
    p = _np.arange(P)[:, None]
    l = _np.arange(S)[None, :]
    j = p % S
    parts = {"ident": _np.eye(P), "quad": p // S == _np.arange(P)[None, :] // S, "dist": l - j, "own": l == j,
             "krow": _np.where(p < ncat, p, p - ncat), "prow": p}
    consts = _np.concatenate([parts[name] for name, _ in CONSTS], axis=1).astype(_np.float32)
    bias = _np.zeros((ncat + E, 2 * D), L0_cond_b.dtype)
    bias[:ncat, :D] = L0_cond_b
    bias[ncat:, D:] = L2_cond_bias

    def by_chunk(w):
        return _np.asarray(w).reshape(F // P, P, -1).transpose(1, 0, 2).reshape(P, -1)

    def expert_t(w):
        return _np.asarray(w).transpose(0, 2, 1).reshape(P, -1)

    spread = lambda w: _np.tile(_np.asarray(w), P // S)[:, None]
    arrays = {
        "x": x,
        "ids": _np.concatenate([itok_B_0_63, itok_B_0_2, itok_B_0_7])[None, :],
        "consts": consts,
        "W0": L0_cond_W,
        "bias": bias,
        "w1": _np.concatenate([L1_cond_W1, spread(L1_cond_b1), spread(L1_cond_v)], axis=1),
        "W2_t": _np.asarray(L2_cond_weight).transpose(2, 0, 1),
        "wi_side": _np.concatenate([_np.asarray(L3_cond_wi).T, expert_t(L3_cond_experts_wi_b),
                                    _np.asarray(L3_cond_experts_wi_a).reshape(P, D).T,
                                    expert_t(L3_cond_experts_wo_b)], axis=1),
        "wo_side": _np.concatenate([by_chunk(_np.asarray(L3_cond_wo).T),
                                    by_chunk(_np.asarray(L3_cond_experts_wo_a).reshape(P, F).T)], axis=1),
        "common": _np.concatenate([L3_cond_common_wi_a, _np.asarray(L3_cond_common_wi_b).T,
                                   L3_cond_common_wo_a, _np.asarray(L3_cond_common_wo_b).T], axis=1),
    }
    arrays = {name: _np.ascontiguousarray(a) for name, a in arrays.items()}
    nc = _bacc.Bacc("TRN2", target_bir_lowering=False, num_devices=1)
    dram = {name: nc.dram_tensor(name + "_dram", a.shape, _mybir.dt.from_np(a.dtype), kind="ExternalInput").ap()
            for name, a in arrays.items()}
    out = nc.dram_tensor("out_dram", tuple(x.shape), _mybir.dt.from_np(_np.dtype("float32")), kind="ExternalOutput").ap()
    build_program(nc, out=out, **dram)
    r = _run(nc, [{name + "_dram": a for name, a in arrays.items()}], core_ids=[0])
    return r.results[0]["out_dram"]
```

```python
from contextlib import ExitStack

import concourse.bass as bass
from concourse import mybir

F32 = mybir.dt.float32
F32R = mybir.dt.float32r
I32 = mybir.dt.int32
BF16 = mybir.dt.bfloat16
ALU = mybir.AluOpType
ACT = mybir.ActivationFunctionType
AX_X = mybir.AxisListType.X

P = 128
ALPHA = 2.0
HIDE = 1e30


FIRST = (("ident", P), ("quad", P), ("dist", 32), ("own", 32), ("prow", 1),
         ("erow", 1), ("b0", P), ("b2", P), ("w1", 32), ("b1", 1), ("v", 1))


def build_program(nc, x, ids, first, W0, W2_t, wi_side, wo_side, common, out):
    B, S, D = x.shape
    NCAT = W0.shape[0]
    A = dict(FIRST)["w1"]
    E = W2_t.shape[1]
    R = common.shape[0]
    F = common.shape[1] // 2 - D
    Q = P // S
    NT = B // Q
    NG = NT // 2
    GB = 2 * Q
    HT = NT // 2
    HB = B // 2
    HN = HT * P
    NC = F // P
    assert F % P == 0 and D == P and S == 32 and A == 32 and E * R == P and HN == 512 and NT == 8 and NC == 4
    KE = 2 * S + E
    CAT, TYPE, EXPERT = (slice(n * B, n * B + B) for n in range(3))
    PG = 3
    SG = GB - PG
    AW = GB + 4

    with ExitStack() as ctx:
        def sb(name, shape, dt=F32):
            return ctx.enter_context(nc.sbuf_tensor(name, shape, dt))

        def sem(name):
            return ctx.enter_context(nc.semaphore(name))

        bank = [ctx.enter_context(nc.psum_tensor(f"bank{i}", [P, 512], F32)) for i in range(8)]
        MIX0 = [bank[2], bank[3], bank[7], bank[5]]
        MIX = [bank[2], bank[3], bank[3], bank[2]]
        MIX2 = [bank[2], bank[3], bank[4], bank[2]]
        TURN1 = [bank[0], bank[1], bank[0], bank[1]]
        TURN = [bank[0], bank[1], bank[0], bank[1]]
        LOW2 = bank[3]
        OUT = [[bank[4][:, :]], [bank[4][:, 0:2 * P], bank[2][:, 0:2 * P]]]
        RING = [bank[6], bank[7], bank[5]]

        first_sb = sb("first_sb", [P, sum(n for _, n in FIRST)])
        cols, at = {}, 0
        for name, n in FIRST:
            cols[name] = first_sb[:, at:at + n]
            at += n
        ident = cols["ident"]
        quad = cols["quad"].rearrange("p (q s) -> p q s", q=Q)
        dist, own = cols["dist"], cols["own"]
        prow, erow = cols["prow"], cols["erow"]
        b0, b2 = cols["b0"][0:NCAT, :], cols["b2"][0:KE, :]
        ids_sb = sb("ids_sb", [P, 3 * B], I32)
        ids_f = sb("ids_f", [P, 3 * B])
        is_cat = sb("is_cat", [NCAT, NT, Q, S])
        is_expert = sb("is_expert", [KE, NT, Q, S], BF16)
        b2_parts = sb("b2_parts", [KE, D], BF16)
        b2_mid = sb("b2_mid", [KE, D], BF16)
        b2_rest = sb("b2_rest", [KE, D])
        ty_own = sb("ty_own", [P, NT, Q])
        ty = sb("ty", [P, NT])
        is_ty = sb("is_ty", [P, 3, NT])
        hide_sign = sb("hide_sign", [P, NT])
        hide_side = sb("hide_side", [P, NT, S])
        hide_own = sb("hide_own", [P, NT, S])
        hidden = sb("hidden", [P, NT, S])
        n_hidden = sb("n_hidden", [P, NT])
        cnt = sb("cnt", [P, NT])
        ex_off = sb("ex_off", [P, B])
        ex_le = sb("ex_le", [P, B])
        ex_mask = sb("ex_mask", [P, B])
        warm = sb("warm", [1, 2])
        busy = sb("busy", [P, 512], BF16)
        w0_sb = sb("w0_sb", [P, B, D])
        v_blocks = sb("v_blocks", [P, Q, S])
        w2_t = sb("w2_t", [P, E, D])
        w2_sel = sb("w2_sel", [P, B, D])
        wi_side_sb = sb("wi_side_sb", [P, 2 * F + 2 * P])
        wo_side_sb = sb("wo_side_sb", [P, 2 * F])
        common_sb = sb("common_sb", [R, 2 * F + 2 * D])
        cwi_a, cwi_b = common_sb[:, 0:D], common_sb[:, D:D + F]
        cwo_a, cwo_b = common_sb[:, D + F:D + 2 * F], common_sb[:, D + 2 * F:]
        wi_sum = sb("wi_sum", [P, F])
        wo_sum = sb("wo_sum", [P, F])
        wide = {"wi": wi_sum[:, :], "ewi_b": wi_side_sb[:, F:2 * F], "small": wi_side_sb[:, 2 * F:],
                "wo": wo_sum[:, :], "ewo_a": wo_side_sb[:, F:2 * F]}
        split = {w: (sb(w + "_hi", [P, a.shape[1]], F32R), sb(w + "_lo", [P, a.shape[1]], F32R))
                 for w, a in wide.items()}
        x0 = sb("x0", [P, NT, D])
        x0_t = sb("x0_t", [P, NT, P])
        x1 = sb("x1", [P, NT, D])
        x1_t = sb("x1_t", [P, NT, P])
        attn = sb("attn", [P, NT, S])
        drop = sb("drop", [P, NT, S])
        least = sb("least", [P, NT])
        probs = sb("probs", [P, NT, S])
        probs_t = sb("probs_t", [P, NT, S])
        den = sb("den", [P, NT])
        den_cnt = sb("den_cnt", [P, NT])
        rden = sb("rden", [P, NT])
        x2 = sb("x2", [P, NT, D])
        x2_t = sb("x2_t", [P, NT, P])
        x3 = sb("x3", [P, NT, D])
        x3_hi = sb("x3_hi", [P, NT * P], F32R)
        x3_lo = sb("x3_lo", [P, NT * P], F32R)
        low = [[sb(f"low{k}{h}", [P, HN]) for h in range(2)] for k in range(2)]
        low_hi = [[sb(f"low{k}_hi{h}", [P, HN], F32R) for h in range(2)] for k in range(2)]
        low_lo = [[sb(f"low{k}_lo{h}", [P, HN], F32R) for h in range(2)] for k in range(2)]
        hid_hi = [sb(f"hid_hi{c}", [P, HN], F32R) for c in range(NC)]
        hid_lo = [sb(f"hid_lo{c}", [P, HN], F32R) for c in range(NC)]
        mlp_t = [sb(f"mlp_t{h}", [P, HN]) for h in range(2)]
        out_sb = sb("out_sb", [P, NT, D])

        x_in = [sem(f"x_in{h}") for h in range(2)]
        w0_in = [sem(f"w0_in{g}") for g in range(NG)]
        w0_in_pool = [sem(f"w0_in_pool{g}") for g in range(NG)]
        ids_in, first_in, w2_in, wi_in, wo_in, common_in = (sem(n) for n in (
            "ids_in", "first_in", "w2_in", "wi_in", "wo_in", "common_in"))
        out_done = sem("out_done")
        w2_sel_pool = sem("w2_sel_pool")
        x0_turned, x1_turned, x2_turned, x3_turned = (sem(f"x{k}_turned") for k in range(4))
        wi_common, wo_common = sem("wi_common"), sem("wo_common")
        l0_done, attn_in, scores_done, pooled, l2_done = (sem(n) for n in (
            "l0_done", "attn_in", "scores_done", "pooled", "l2_done"))
        low_done, hid_done, low2_done, mlp_done, mlp_turned = (sem(n) for n in (
            "low_done", "hid_done", "low2_done", "mlp_done", "mlp_turned"))
        hid_used = sem("hid_used")
        x1_t_ready, x2_t_ready, x3_hi_ready = (sem(n) for n in ("x1_t_ready", "x2_t_ready", "x3_hi_ready"))
        warm_done, w2_sel_act, x0_t_ready_act, attn_ready, exp_ready = (sem(n) for n in (
            "warm_done", "w2_sel_act", "x0_t_ready_act", "attn_ready", "exp_ready"))
        hi_ready = {w: sem(w + "_hi_ready") for w in wide}
        low_hi_ready, hid_hi_ready, low2_hi_ready, mlp_copied = (sem(n) for n in (
            "low_hi_ready", "hid_hi_ready", "low2_hi_ready", "mlp_copied"))
        x0_t_ready, idf_ready, cat_ready, expert_ready, b2_step, b2_ready = (sem(n) for n in (
            "x0_t_ready", "idf_ready", "cat_ready", "expert_ready", "b2_step", "b2_ready"))
        ex_step, ex_ready, ty_step, mask_step, warm_ready = (sem(n) for n in (
            "ex_step", "ex_ready", "ty_step", "mask_step", "warm_ready"))
        mask_ready, cnt_step, cnt_ready, v_ready, wi_summed, wo_summed = (sem(n) for n in (
            "mask_ready", "cnt_step", "cnt_ready", "v_ready", "wi_summed", "wo_summed"))
        lo_ready = {w: sem(w + "_lo_ready") for w in wide}
        busy_ready, x1_ready, masked, least_ready = (sem(n) for n in (
            "busy_ready", "x1_ready", "masked", "least_ready"))
        probs_ready, den_ready, rden_ready, x2_ready, x3_ready, x3_lo_ready = (sem(n) for n in (
            "probs_ready", "den_ready", "rden_ready", "x2_ready", "x3_ready", "x3_lo_ready"))
        low_m, low_lo_ready, hid_lo_ready, low2_m, low2_lo_ready, out_ready = (sem(n) for n in (
            "low_m", "low_lo_ready", "hid_lo_ready", "low2_m", "low2_lo_ready", "out_ready"))

        def tiles(g):
            return slice(2 * g, 2 * g + 2)

        def group_bank(b, w=P):
            return b[:, 0:2 * w].rearrange("p (t n) -> p t n", t=2)

        x_tok = x.rearrange("b s d -> (b s) d").rearrange("(t p) d -> p t d", p=P)
        out_tok = out.rearrange("b s d -> (b s) d").rearrange("(t p) d -> p t d", p=P)

        def gather_w0(eng, regs, b_first, landed):
            for k, reg in enumerate(regs):
                cat = eng.snap(reg, min_val=0, max_val=NCAT - 1)
                eng.dma_start(w0_sb[:, b_first + k, :], W0[bass.ds(cat, 1), :, :].rearrange("o d h -> (o d) h"))\
                   .then_inc(landed, 16)

        block = ctx.enter_context(nc.Block())

        @block.sync
        def _(sp):
            regs = [sp.alloc_register(f"sp_cat{k}") for k in range(GB + SG)]
            sp.load(regs, ids[0:1, 0:GB + SG])
            for g in range(NG):
                if g == 2:
                    sp.wait_ge(ids_in, 16)
                if g >= 2:
                    sp.load(regs[GB * (g % 2):GB * (g % 2) + SG], ids_sb[0:1, GB * g:GB * g + SG])
                gather_w0(sp, regs[GB * (g % 2):GB * (g % 2) + SG], GB * g, w0_in[g])
                if g == 1:
                    sp.dma_start(common_sb[:, :], common).then_inc(common_in, 16)
                    sp.dma_start(w2_t[:, :, :], W2_t).then_inc(w2_in, 16)
                    sp.dma_start(wi_side_sb[:, :], wi_side).then_inc(wi_in, 16)
            sp.dma_start(wo_side_sb[:, :], wo_side).then_inc(wo_in, 16)
            for g in range(NG):
                sp.wait_ge(out_ready, g + 1)
                sp.dma_start(out_tok[:, tiles(g), :], out_sb[:, tiles(g), :]).then_inc(out_done, 16)
            sp.wait_ge(out_done, 16 * NG)

        @block.gpsimd
        def _(pool):
            regs = [[pool.alloc_register(f"pool_cat{g}_{k}") for k in range(PG)] for g in range(2)]
            pool.load(regs[0], ids[0:1, SG:GB])
            gather_w0(pool, regs[0], SG, w0_in_pool[0])
            pool.wait_ge(ids_in, 16)
            for g in range(1, NG):
                pool.load(regs[g % 2], ids_sb[0:1, GB * g + SG:GB * g + GB])
                gather_w0(pool, regs[g % 2], GB * g + SG, w0_in_pool[g])
            ex_regs = [[pool.alloc_register(f"pool_ex{i}_{k}") for k in range(n)]
                       for i, n in enumerate((GB, 2 * GB - AW))]

            def select_w2(g):
                regs = ex_regs[g == 1]
                first = AW if g == 1 else GB * g
                pool.load(regs, ids_sb[0:1, 2 * B + first:2 * B + GB * g + GB])
                for k, reg in enumerate(regs, first):
                    e = pool.snap(reg, min_val=0, max_val=E - 1)
                    pool.tensor_copy(w2_sel[:, k, :], w2_t[:, bass.ds(e, 1), :].rearrange("p o n -> p (o n)"))\
                        .then_inc(w2_sel_pool, 1)

            def weight_low(w):
                pool.wait_ge(hi_ready[w], 1)
                pool.tensor_tensor(split[w][1][:, :], wide[w], split[w][0][:, :].bitcast(F32), ALU.subtract)\
                    .then_inc(lo_ready[w], 1)

            pool.wait_ge(w2_in, 16)
            select_w2(1)
            weight_low("wi")
            weight_low("ewi_b")
            select_w2(2)
            weight_low("ewo_a")
            select_w2(3)
            weight_low("wo")

        @block.tensor
        def _(pe):
            def turn_x(src, g, b, done):
                for k in range(2):
                    mm = pe.transpose(b[:, k * P:k * P + P], src[:, 2 * g + k, :], ident)
                mm.then_inc(done, 1)

            def keep_busy(n, b):
                for _ in range(n):
                    pe.matmul(b[:, :], busy[:, 0:P], busy[:, :], start=True, stop=True, skip_group_check=True)

            def turn_x0(h):
                pe.wait_ge(x_in[h], 16)
                for k in range(HT):
                    mm = pe.transpose(bank[5][:, k * P:k * P + P], x0[:, HT * h + k, :], ident)
                mm.then_inc(x0_turned, 1)

            def add_bias(g, b, one_hot, rows):
                for t in range(2):
                    pe.matmul(b[:, t * D:t * D + D], one_hot[:, 2 * g + t, :, :].rearrange("k q s -> k (q s)"),
                              rows, start=t == 0, stop=False, skip_group_check=True)

            def add_b0(g):
                pe.wait_ge(cat_ready, 1 + g // 2)
                add_bias(g, MIX0[g], is_cat, b0)

            def add_b2(g):
                pe.wait_ge(expert_ready, 1 + g // 2)
                pe.wait_ge(b2_ready, 1)
                add_bias(g, MIX2[g], is_expert, b2_parts[:, :])

            def rows_times(src_t, w, b, g, done):
                for k in range(2):
                    for q in range(Q):
                        t = 2 * g + k
                        mm = pe.matmul(b[q * S:q * S + S, k * D:k * D + D], src_t[:, t, q * S:q * S + S],
                                       w[:, Q * t + q, :], start=False, stop=True, skip_group_check=True)
                mm.then_inc(done, 1)

            def layer0(g):
                pe.wait_ge(w0_in[g], 16 * SG)
                pe.wait_ge(w0_in_pool[g], 16 * PG)
                pe.wait_ge((x0_t_ready, x0_t_ready_act)[g // 2], 1)
                rows_times(x0_t, w0_sb, MIX0[g], g, l0_done)

            def turn_x1(g):
                pe.wait_ge(x1_ready, g + 1)
                turn_x(x1, g, TURN1[g], x1_turned)

            def attn_product(g):
                pe.wait_ge(x1_t_ready, g + 1)
                for q in range(Q):
                    mm = pe.matmul(MIX[g][q * S:q * S + S, 0:2 * S].rearrange("p (t l) -> p t l", t=2),
                                   cols["w1"], x1_t[:, tiles(g), q * S:q * S + S], start=True, stop=True)
                mm.then_inc(attn_in, 1)

            def score_product(g):
                pe.wait_ge(attn_ready, g + 1)
                pe.wait_ge(v_ready, 1)
                for q in range(Q):
                    mm = pe.matmul(MIX[g][q * S:q * S + S, 0:2 * S].rearrange("p (t l) -> p t l", t=2),
                                   v_blocks[:, q, :], attn[:, tiles(g), :], start=True, stop=True)
                mm.then_inc(scores_done, 1)

            def pool_rows(g):
                pe.wait_ge(probs_ready, g + 1)
                for k in range(2):
                    for q in range(Q):
                        c = slice(q * S, q * S + S)
                        mm = pe.matmul(MIX[g][c, k * D:k * D + D], probs_t[c, 2 * g + k, :], x1[c, 2 * g + k, :],
                                       start=True, stop=True, skip_group_check=True)
                mm.then_inc(pooled, 1)

            def turn_x2(g):
                pe.wait_ge(x2_ready, 2 * (g + 1))
                turn_x(x2, g, TURN[g], x2_turned)

            def layer2(g):
                pe.wait_ge(x2_t_ready, g + 1)
                pe.wait_ge(w2_sel_act, AW if g else GB)
                if g:
                    pe.wait_ge(w2_sel_pool, GB * (g + 1) - AW)
                rows_times(x2_t, w2_sel, MIX2[g], g, l2_done)

            def turn_x3(g):
                pe.wait_ge(x3_ready, g + 1)
                turn_x(x3, g, TURN[g], x3_turned)

            def three(acc, w, col, hi, lo, first, last):
                w_hi, w_lo = split[w]
                c = slice(col * P, col * P + P)
                pe.matmul(acc, w_hi[:, c], hi, start=first, stop=False, skip_group_check=True)
                pe.matmul(acc, w_hi[:, c], lo, start=False, stop=False, skip_group_check=True)
                return pe.matmul(acc, w_lo[:, c], hi, start=False, stop=last, skip_group_check=True)

            def ring(h, k):
                return RING[(5 * h + k) % 3][:, :]

            def half(a, h):
                return a[:, HN * h:HN * h + HN]

            def wait_ring(h, k):
                n = 5 * h + k - 3
                if n in (0, 5):
                    pe.wait_ge(low_m, n // 5 + 1)
                elif n > 0:
                    pe.wait_ge(hid_lo_ready, n - n // 5)

            def low_rank(h):
                wait_ring(h, 0)
                pe.wait_ge(x3_hi_ready, 2 * (h + 1))
                pe.wait_ge(x3_lo_ready, 2 * (h + 1))
                three(ring(h, 0), "small", 0, half(x3_hi, h), half(x3_lo, h), True, True).then_inc(low_done, 1)

            def hidden_dense(h, c):
                wait_ring(h, c + 1)
                three(ring(h, c + 1), "wi", c, half(x3_hi, h), half(x3_lo, h), True, False)

            def hidden_low(h, c):
                if c == 0:
                    pe.wait_ge(low_hi_ready, h + 1)
                    pe.wait_ge(low_lo_ready, h + 1)
                three(ring(h, c + 1), "ewi_b", c, low_hi[0][h][:, :], low_lo[0][h][:, :], False, True)\
                    .then_inc(hid_done, 1)

            def out_low(h, c):
                pe.wait_ge(hid_hi_ready, 4 * h + c + 1)
                pe.wait_ge(hid_lo_ready, 4 * h + c + 1)
                if c == 0 and h == 1:
                    pe.wait_ge(low2_m, 1)
                mm = three(LOW2[:, :], "ewo_a", c, hid_hi[c][:, :], hid_lo[c][:, :], c == 0, c == NC - 1)
                if c == NC - 1:
                    mm.then_inc(low2_done, 1)

            def out_parts(h):
                w = HN // len(OUT[h])
                return [(acc, slice(i * w, i * w + w)) for i, acc in enumerate(OUT[h])]

            def out_dense(h, c):
                if c == 0 and h == 1:
                    pe.wait_ge(mlp_copied, 2)
                for acc, t in out_parts(h):
                    mm = three(acc, "wo", c, hid_hi[c][:, t], hid_lo[c][:, t], c == 0, False)
                mm.then_inc(hid_used, 1)

            def out_expert(h):
                for n, (acc, t) in enumerate(out_parts(h), 1 + h):
                    pe.wait_ge(low2_hi_ready, n)
                    pe.wait_ge(low2_lo_ready, n)
                    three(acc, "small", 1, low_hi[1][h][:, t], low_lo[1][h][:, t], False, True).then_inc(mlp_done, 1)

            def turn_mlp(h):
                pe.wait_ge(x3_lo_ready, NG)
                for g in (2 * h, 2 * h + 1):
                    pe.wait_ge(mlp_copied, g + 1)
                    if h == 1:
                        pe.wait_ge(out_ready, g - 1)
                    for k in range(2):
                        t = 2 * (g % 2) + k
                        mm = pe.transpose(TURN[g][:, k * P:k * P + P], mlp_t[h][:, t * P:t * P + P], ident)
                    mm.then_inc(mlp_turned, 1)

            def common_wi(c):
                mm = pe.matmul(bank[6][:, c * P:c * P + P], cwi_a, cwi_b[:, c * P:c * P + P], start=True, stop=True)
                if c == NC - 1:
                    mm.then_inc(wi_common, 1)

            def common_wo(c):
                mm = pe.matmul(bank[4][:, c * P:c * P + P], cwo_a[:, c * P:c * P + P], cwo_b, start=True, stop=True)
                if c == NC - 1:
                    mm.then_inc(wo_common, 1)

            pe.wait_ge(busy_ready, 1)
            keep_busy(9, bank[0])
            pe.wait_ge(first_in, 16)
            turn_x0(0)
            add_b0(0)
            layer0(0)
            add_b0(1)
            turn_x1(0)
            add_b0(2)
            attn_product(0)
            keep_busy(2, bank[1])
            layer0(1)
            score_product(0)
            pe.wait_ge(x0_t_ready, 1)
            turn_x0(1)
            turn_x1(1)
            pe.wait_ge(common_in, 16)
            common_wi(0)
            common_wi(1)
            attn_product(1)
            keep_busy(2, bank[0])
            score_product(1)
            pool_rows(0)
            common_wi(2)
            common_wi(3)
            keep_busy(2, bank[0])
            turn_x2(0)
            pool_rows(1)
            add_b2(0)
            layer2(0)
            turn_x2(1)
            add_b2(1)
            pe.wait_ge(x0_t_ready_act, 1)
            add_b0(3)
            layer2(1)
            turn_x3(0)
            common_wo(0)
            common_wo(1)
            turn_x3(1)
            layer0(2)
            layer0(3)
            pe.wait_ge(hi_ready["small"], 1)
            pe.wait_ge(lo_ready["small"], 1)
            low_rank(0)
            turn_x1(2)
            pe.wait_ge(hi_ready["wi"], 1)
            pe.wait_ge(lo_ready["wi"], 1)
            hidden_dense(0, 0)
            common_wo(2)
            common_wo(3)
            pe.wait_ge(x3_ready, 2)
            attn_product(2)
            pe.wait_ge(x1_ready, 4)
            hidden_dense(0, 1)
            score_product(2)
            pe.wait_ge(x3_lo_ready, 2)
            turn_x1(3)
            hidden_dense(0, 2)
            attn_product(3)
            pe.wait_ge(hi_ready["ewi_b"], 1)
            pe.wait_ge(lo_ready["ewi_b"], 1)
            hidden_low(0, 0)
            score_product(3)
            hidden_low(0, 1)
            pool_rows(2)
            hidden_low(0, 2)
            hidden_dense(0, 3)
            turn_x2(2)
            pe.wait_ge(wo_summed, 1)
            add_b2(2)
            hidden_low(0, 3)
            layer2(2)
            pe.wait_ge(hi_ready["ewo_a"], 1)
            pe.wait_ge(lo_ready["ewo_a"], 1)
            out_low(0, 0)
            pool_rows(3)
            turn_x3(2)
            out_low(0, 1)
            out_low(0, 2)
            turn_x2(3)
            add_b2(3)
            out_low(0, 3)
            layer2(3)
            pe.wait_ge(hi_ready["wo"], 1)
            pe.wait_ge(lo_ready["wo"], 1)
            out_dense(0, 0)
            turn_x3(3)
            out_dense(0, 1)
            out_dense(0, 2)
            out_dense(0, 3)
            low_rank(1)
            out_expert(0)
            for c in range(3):
                hidden_dense(1, c)
            for c in range(3):
                hidden_low(1, c)
            turn_mlp(0)
            out_low(1, 0)
            hidden_dense(1, 3)
            hidden_low(1, 3)
            out_low(1, 1)
            out_low(1, 2)
            out_dense(1, 0)
            out_low(1, 3)
            for c in range(1, NC):
                out_dense(1, c)
            out_expert(1)
            turn_mlp(1)

        @block.scalar
        def _(act):
            regs = [act.alloc_register(f"act_ex{k}") for k in range(AW)]

            def copy_turned(dst, b, g, turned, ready):
                act.wait_ge(turned, g + 1)
                act.copy(dst[:, tiles(g), :].rearrange("p t n -> p (t n)"), b[:, 0:2 * P]).then_inc(ready, 1)

            def select_w2(first, last):
                for k in range(first, last):
                    e = act.snap(regs[k], min_val=0, max_val=E - 1)
                    act.copy(w2_sel[:, k, :], w2_t[:, bass.ds(e, 1), :].rearrange("p o n -> p (o n)"))\
                       .then_inc(w2_sel_act, 1)

            def copy_x0():
                act.wait_ge(x0_turned, 2)
                act.copy(x0_t[:, HT:NT, :].rearrange("p t n -> p (t n)"), bank[5][:, :]).then_inc(x0_t_ready_act, 1)

            def attn_tanh(g):
                act.wait_ge(attn_in, g + 1)
                act.activation(attn[:, tiles(g), :].rearrange("p t l -> p (t l)"), MIX[g][:, 0:2 * S], ACT.Tanh,
                               bias=cols["b1"]).then_inc(attn_ready, 1)

            def exp_scores(g):
                act.wait_ge(least_ready, g + 1)
                for t in (2 * g, 2 * g + 1):
                    act.activation(probs[:, t, :], drop[:, t, :], ACT.Exp, bias=least[:, t:t + 1], scale=-1.0)\
                       .then_inc(exp_ready, 1)

            def x3_high(g):
                act.wait_ge(x3_turned, g + 1)
                act.copy(x3_hi[:, 2 * P * g:2 * P * (g + 1)], TURN[g][:, 0:2 * P]).then_inc(x3_hi_ready, 1)

            def weight_high(w):
                act.copy(split[w][0][:, :], wide[w]).then_inc(hi_ready[w], 1)

            def low_high(k, h, m, ready, parts=1):
                for i in range(parts):
                    act.wait_ge(m, h + 1 + i)
                    c = slice(i * HN // parts, (i + 1) * HN // parts)
                    act.copy(low_hi[k][h][:, c], low[k][h][:, c]).then_inc(ready, 1)

            def hidden_high(h, c):
                act.wait_ge(hid_done, 4 * h + c + 1)
                if h == 1:
                    act.wait_ge(hid_used, c + 1)
                act.activation(hid_hi[c][:, :], RING[(5 * h + c + 1) % 3][:, :], ACT.Relu).then_inc(hid_hi_ready, 1)

            def copy_mlp(h):
                for k in range(2):
                    c = slice(2 * P * k, 2 * P * (k + 1))
                    act.wait_ge(mlp_done, 1 + (1 + k) * h)
                    act.copy(mlp_t[h][:, c], OUT[0][0][:, c] if h == 0 else OUT[1][k]).then_inc(mlp_copied, 1)

            act.dma_start(ids_sb[:, :], ids.partition_broadcast(P)).then_inc(ids_in, 16)
            act.dma_start(first_sb[:, :], first).then_inc(first_in, 16)
            act.dma_start(x0[:, 0:HT, :], x_tok[:, 0:HT, :]).then_inc(x_in[0], 16)
            act.wait_ge(warm_ready, 1)
            act.activation(warm[:, 1:2], warm[:, 0:1], ACT.Exp).then_inc(warm_done, 1)
            act.wait_ge(x_in[0], 16)
            act.dma_start(x0[:, HT:NT, :], x_tok[:, HT:NT, :]).then_inc(x_in[1], 16)
            act.wait_ge(ids_in, 16)
            act.load(regs, ids_sb[0:1, 2 * B:2 * B + AW])
            copy_turned(x1_t, TURN1[0], 0, x1_turned, x1_t_ready)
            attn_tanh(0)
            copy_turned(x1_t, TURN1[1], 1, x1_turned, x1_t_ready)
            exp_scores(0)
            attn_tanh(1)
            act.wait_ge(w2_in, 16)
            select_w2(0, 5)
            exp_scores(1)
            select_w2(5, GB)
            copy_turned(x2_t, TURN[0], 0, x2_turned, x2_t_ready)
            copy_x0()
            select_w2(GB, AW)
            act.wait_ge(wi_in, 16)
            weight_high("small")
            copy_turned(x2_t, TURN[1], 1, x2_turned, x2_t_ready)
            act.wait_ge(wi_summed, 1)
            weight_high("wi")
            x3_high(0)
            weight_high("ewi_b")
            x3_high(1)
            copy_turned(x1_t, TURN1[2], 2, x1_turned, x1_t_ready)
            low_high(0, 0, low_m, low_hi_ready)
            attn_tanh(2)
            act.wait_ge(wo_in, 16)
            weight_high("ewo_a")
            act.wait_ge(wo_summed, 1)
            weight_high("wo")
            copy_turned(x1_t, TURN1[3], 3, x1_turned, x1_t_ready)
            exp_scores(2)
            attn_tanh(3)
            hidden_high(0, 0)
            hidden_high(0, 1)
            copy_turned(x2_t, TURN[2], 2, x2_turned, x2_t_ready)
            exp_scores(3)
            hidden_high(0, 2)
            hidden_high(0, 3)
            x3_high(2)
            copy_turned(x2_t, TURN[3], 3, x2_turned, x2_t_ready)
            x3_high(3)
            low_high(1, 0, low2_m, low2_hi_ready)
            low_high(0, 1, low_m, low_hi_ready)
            copy_mlp(0)
            for c in range(NC):
                hidden_high(1, c)
            low_high(1, 1, low2_m, low2_hi_ready, parts=2)
            copy_mlp(1)

        @block.vector
        def _(dve):
            def copy_x0():
                dve.wait_ge(x0_turned, 1)
                dve.tensor_copy(x0_t[:, 0:HT, :].rearrange("p t n -> p (t n)"), bank[5][:, :]).then_inc(x0_t_ready, 1)

            def make_x1(g):
                dve.wait_ge(l0_done, g + 1)
                dve.wait_ge(x_in[g // 2], 16)
                dve.tensor_tensor(x1[:, tiles(g), :], group_bank(MIX0[g]), x0[:, tiles(g), :], ALU.add)\
                   .then_inc(x1_ready, 1)

            def mask_scores(g):
                t = tiles(g)
                dve.wait_ge(scores_done, g + 1)
                dve.scalar_tensor_tensor(out=drop[:, t, :], in0=hidden[:, t, :], scalar=HIDE,
                                         in1=group_bank(MIX[g], S), op0=ALU.mult, op1=ALU.subtract).then_inc(masked, 1)
                dve.wait_ge(masked, g + 1)
                dve.tensor_reduce(least[:, t], drop[:, t, :], AX_X, ALU.min).then_inc(least_ready, 1)

            def turn_probs(g):
                t = tiles(g)
                dve.wait_ge(exp_ready, 2 * (g + 1))
                dve.transpose(probs_t[:, t, :].rearrange("p t j -> p (t j)"),
                              probs[:, t, :].rearrange("p t l -> p (t l)")).then_inc(probs_ready, 1)
                dve.tensor_reduce(den[:, t], probs[:, t, :], AX_X, ALU.add).then_inc(den_ready, 1)
                dve.wait_ge(den_ready, 2 * g + 1)
                dve.tensor_tensor(den_cnt[:, t], den[:, t], cnt[:, t], ALU.mult).then_inc(den_ready, 1)
                dve.wait_ge(den_ready, 2 * g + 2)
                dve.reciprocal(rden[:, t], den_cnt[:, t]).then_inc(rden_ready, 1)

            def make_x2(g):
                dve.wait_ge(pooled, g + 1)
                dve.wait_ge(rden_ready, g + 1)
                for k in range(2):
                    dve.scalar_tensor_tensor(out=x2[:, 2 * g + k, :], in0=MIX[g][:, k * D:k * D + D],
                                             scalar=rden[:, 2 * g + k:2 * g + k + 1], in1=x1[:, 2 * g + k, :],
                                             op0=ALU.mult, op1=ALU.add).then_inc(x2_ready, 1)

            def make_x3(g):
                dve.wait_ge(l2_done, g + 1)
                dve.tensor_tensor(x3[:, tiles(g), :], group_bank(MIX2[g]), x2[:, tiles(g), :], ALU.add)\
                   .then_inc(x3_ready, 1)

            def x3_low(g):
                c = slice(2 * P * g, 2 * P * (g + 1))
                dve.wait_ge(x3_hi_ready, g + 1)
                dve.tensor_tensor(x3_lo[:, c], TURN[g][:, 0:2 * P], x3_hi[:, c].bitcast(F32), ALU.subtract)\
                   .then_inc(x3_lo_ready, 1)

            def add_common(w_sum, w_t, b, done, ready):
                dve.wait_ge(done, 1)
                dve.scalar_tensor_tensor(out=w_sum[:, :], in0=b[:, :], scalar=ALPHA, in1=w_t[:, 0:F],
                                         op0=ALU.mult, op1=ALU.add).then_inc(ready, 1)

            def weight_low(w):
                dve.wait_ge(hi_ready[w], 1)
                dve.tensor_tensor(split[w][1][:, :], wide[w], split[w][0][:, :].bitcast(F32), ALU.subtract)\
                   .then_inc(lo_ready[w], 1)

            def mask_low(k, h, b, done, m, parts=1):
                dve.wait_ge(done, h + 1)
                n = HB // parts
                for i in range(parts):
                    first = HB * h + i * n
                    c = slice(i * n * S, (i + 1) * n * S)
                    dve.tensor_tensor(low[k][h][:, c].rearrange("p (b s) -> p b s", s=S),
                                      b[:, c].rearrange("p (b s) -> p b s", s=S),
                                      ex_mask[:, first:first + n].unsqueeze(2).to_broadcast([P, n, S]),
                                      ALU.mult).then_inc(m, 1)

            def low_low(k, h, hi_ready, ready, parts=1):
                for i in range(parts):
                    dve.wait_ge(hi_ready, h + 1 + i)
                    c = slice(i * HN // parts, (i + 1) * HN // parts)
                    dve.tensor_tensor(low_lo[k][h][:, c], low[k][h][:, c], low_hi[k][h][:, c].bitcast(F32),
                                      ALU.subtract).then_inc(ready, 1)

            def hidden_lo(h, c):
                dve.wait_ge(hid_hi_ready, 4 * h + c + 1)
                dve.scalar_tensor_tensor(out=hid_lo[c][:, :], in0=RING[(5 * h + c + 1) % 3][:, :], scalar=0.0,
                                         in1=hid_hi[c][:, :].bitcast(F32), op0=ALU.max, op1=ALU.subtract)\
                   .then_inc(hid_lo_ready, 1)

            def finish(h):
                for g in (2 * h, 2 * h + 1):
                    dve.wait_ge(mlp_turned, g + 1)
                    dve.tensor_tensor(out_sb[:, tiles(g), :], group_bank(TURN[g]), x3[:, tiles(g), :],
                                      ALU.add).then_inc(out_ready, 1)

            def one_hot(dst, h, ids, row, n, ready):
                first = ids.start + HB * h
                dve.tensor_scalar(dst[:, HT * h:HT * h + HT, :, :].rearrange("p t q s -> p (t q) s"),
                                  ids_f[0:n, first:first + HB].unsqueeze(2).to_broadcast([n, HB, S]),
                                  row[0:n, :], None, ALU.is_equal).then_inc(ready, 1)

            dve.memset(busy[:, :], 0.0).then_inc(busy_ready, 1)
            dve.memset(warm[:, 0:1], 0.0).then_inc(warm_ready, 1)
            dve.wait_ge(ids_in, 16)
            dve.tensor_copy(ids_f[:, :], ids_sb[:, :]).then_inc(idf_ready, 1)
            dve.wait_ge(first_in, 16)
            dve.wait_ge(idf_ready, 1)
            for h in range(2):
                one_hot(is_cat, h, CAT, prow, NCAT, cat_ready)
            dve.tensor_scalar(v_blocks[:, :, :], quad, cols["v"], None, ALU.mult).then_inc(v_ready, 1)
            dve.tensor_tensor(ty_own[:, :, :], ids_f[:, TYPE].rearrange("p (t q) -> p t q", q=Q),
                              quad[:, :, 0].unsqueeze(1).to_broadcast([P, NT, Q]), ALU.mult).then_inc(ty_step, 1)
            one_hot(is_expert, 0, EXPERT, erow, KE, expert_ready)
            dve.tensor_copy(b2_parts[:, :], b2).then_inc(b2_step, 1)
            copy_x0()
            dve.wait_ge(ty_step, 1)
            dve.tensor_reduce(ty[:, :], ty_own[:, :, :], AX_X, ALU.add).then_inc(ty_step, 1)
            dve.wait_ge(ty_step, 2)
            for n, op in enumerate((ALU.is_equal, ALU.is_equal, ALU.is_ge)):
                dve.tensor_scalar(is_ty[:, n, :], ty[:, :], float(n), None, op).then_inc(ty_step, 1)
            dve.wait_ge(ty_step, 5)
            dve.tensor_tensor(hide_sign[:, :], is_ty[:, 0, :], is_ty[:, 1, :], ALU.subtract).then_inc(mask_step, 1)
            make_x1(0)
            dve.wait_ge(mask_step, 1)
            dve.tensor_tensor(hide_side[:, :, :], hide_sign[:, :].unsqueeze(2).to_broadcast([P, NT, S]),
                              dist.unsqueeze(1).to_broadcast([P, NT, S]), ALU.mult).then_inc(mask_step, 1)
            dve.tensor_tensor(hide_own[:, :, :], is_ty[:, 2, :].unsqueeze(2).to_broadcast([P, NT, S]),
                              own.unsqueeze(1).to_broadcast([P, NT, S]), ALU.mult).then_inc(mask_step, 1)
            dve.wait_ge(mask_step, 3)
            dve.scalar_tensor_tensor(out=hidden[:, :, :], in0=hide_side[:, :, :], scalar=0.0, in1=hide_own[:, :, :],
                                     op0=ALU.is_gt, op1=ALU.add).then_inc(mask_ready, 1)
            dve.wait_ge(mask_ready, 1)
            dve.tensor_reduce(n_hidden[:, :], hidden[:, :, :], AX_X, ALU.add).then_inc(cnt_step, 1)
            dve.wait_ge(cnt_step, 1)
            dve.tensor_scalar(cnt[:, :], n_hidden[:, :], -1.0, float(S), ALU.mult, ALU.add).then_inc(cnt_ready, 1)
            dve.wait_ge(b2_step, 1)
            dve.tensor_tensor(b2_rest[:, :], b2, b2_parts[:, :], ALU.subtract).then_inc(b2_step, 1)
            make_x1(1)
            mask_scores(0)
            dve.wait_ge(b2_step, 2)
            dve.tensor_copy(b2_mid[:, :], b2_rest[:, :]).then_inc(b2_step, 1)
            dve.tensor_copy(b2_parts[S:2 * S, :], b2_rest[S:2 * S, :]).then_inc(b2_step, 1)
            dve.wait_ge(b2_step, 4)
            dve.tensor_tensor(b2_parts[2 * S:KE, :], b2_rest[2 * S:KE, :], b2_mid[2 * S:KE, :], ALU.subtract)\
               .then_inc(b2_ready, 1)
            dve.wait_ge(cnt_ready, 1)
            turn_probs(0)
            mask_scores(1)
            make_x2(0)
            turn_probs(1)
            make_x2(1)
            dve.wait_ge(wi_in, 16)
            add_common(wi_sum, wi_side_sb, bank[6], wi_common, wi_summed)
            make_x3(0)
            weight_low("small")
            dve.tensor_scalar(ex_off[:, :], ids_f[:, EXPERT], float(R), prow, ALU.mult, ALU.subtract)\
               .then_inc(ex_step, 1)
            one_hot(is_expert, 1, EXPERT, erow, KE, expert_ready)
            make_x3(1)
            x3_low(0)
            dve.wait_ge(ex_step, 1)
            dve.tensor_scalar(ex_le[:, :], ex_off[:, :], 0.0, ALPHA, ALU.is_le, ALU.mult).then_inc(ex_step, 1)
            x3_low(1)
            make_x1(2)
            make_x1(3)
            dve.wait_ge(ex_step, 2)
            dve.scalar_tensor_tensor(out=ex_mask[:, :], in0=ex_off[:, :], scalar=float(1 - R), in1=ex_le[:, :],
                                     op0=ALU.is_ge, op1=ALU.mult).then_inc(ex_ready, 1)
            dve.wait_ge(ex_ready, 1)
            mask_low(0, 0, RING[0], low_done, low_m)
            dve.wait_ge(wo_in, 16)
            add_common(wo_sum, wo_side_sb, bank[4], wo_common, wo_summed)
            low_low(0, 0, low_hi_ready, low_lo_ready)
            mask_scores(2)
            turn_probs(2)
            hidden_lo(0, 0)
            make_x2(2)
            mask_scores(3)
            hidden_lo(0, 1)
            turn_probs(3)
            hidden_lo(0, 2)
            make_x3(2)
            make_x2(3)
            hidden_lo(0, 3)
            x3_low(2)
            make_x3(3)
            mask_low(1, 0, LOW2, low2_done, low2_m)
            x3_low(3)
            low_low(1, 0, low2_hi_ready, low2_lo_ready)
            mask_low(0, 1, RING[2], low_done, low_m)
            low_low(0, 1, low_hi_ready, low_lo_ready)
            for c in range(3):
                hidden_lo(1, c)
            finish(0)
            hidden_lo(1, 3)
            mask_low(1, 1, LOW2, low2_done, low2_m, parts=2)
            low_low(1, 1, low2_hi_ready, low2_lo_ready, parts=2)
            finish(1)


def kernel(x, itok_B_0_63, itok_B_0_2, itok_B_0_7, L0_cond_W, L0_cond_b, L1_cond_W1, L1_cond_b1, L1_cond_v,
           L2_cond_weight, L2_cond_bias, L3_cond_wi, L3_cond_wo, L3_cond_common_wi_a, L3_cond_common_wi_b,
           L3_cond_common_wo_a, L3_cond_common_wo_b, L3_cond_experts_wi_a, L3_cond_experts_wi_b,
           L3_cond_experts_wo_a, L3_cond_experts_wo_b):
    import numpy as _np
    import concourse.bacc as _bacc
    from concourse import mybir as _mybir
    from concourse.bass_utils import run_bass_kernel_spmd as _run

    S = x.shape[1]
    ncat, D = L0_cond_b.shape
    E = L2_cond_bias.shape[0]
    F = L3_cond_wi.shape[0]
    p = _np.arange(P)[:, None]
    l = _np.arange(S)[None, :]
    j = p % S
    repeat = lambda w: _np.tile(_np.asarray(w), P // S)[:, None]
    b0 = _np.zeros((P, D), L0_cond_b.dtype)
    b0[:ncat] = L0_cond_b
    b2 = _np.zeros((P, D), L2_cond_bias.dtype)
    erow = _np.full((P, 1), -1)
    for q in range(3):
        b2[q * S:q * S + E] = L2_cond_bias
        erow[q * S:q * S + E, 0] = _np.arange(E)
    parts = {"ident": _np.eye(P), "quad": p // S == _np.arange(P)[None, :] // S, "dist": l - j, "own": l == j,
             "prow": p,
             "erow": erow, "b0": b0, "b2": b2, "w1": L1_cond_W1, "b1": repeat(L1_cond_b1), "v": repeat(L1_cond_v)}

    def by_chunk(w):
        return _np.asarray(w).reshape(F // P, P, -1).transpose(1, 0, 2).reshape(P, -1)

    def expert_t(w):
        return _np.asarray(w).transpose(0, 2, 1).reshape(P, -1)

    arrays = {
        "x": x,
        "ids": _np.concatenate([itok_B_0_63, itok_B_0_2, itok_B_0_7])[None, :],
        "first": _np.concatenate([_np.asarray(parts[name], _np.float32) for name, _ in FIRST], axis=1),
        "W0": L0_cond_W,
        "W2_t": _np.asarray(L2_cond_weight).transpose(2, 0, 1),
        "wi_side": _np.concatenate([_np.asarray(L3_cond_wi).T, expert_t(L3_cond_experts_wi_b),
                                    _np.asarray(L3_cond_experts_wi_a).reshape(P, D).T,
                                    expert_t(L3_cond_experts_wo_b)], axis=1),
        "wo_side": _np.concatenate([by_chunk(_np.asarray(L3_cond_wo).T),
                                    by_chunk(_np.asarray(L3_cond_experts_wo_a).reshape(P, F).T)], axis=1),
        "common": _np.concatenate([L3_cond_common_wi_a, _np.asarray(L3_cond_common_wi_b).T,
                                   L3_cond_common_wo_a, _np.asarray(L3_cond_common_wo_b).T], axis=1),
    }
    arrays = {name: _np.ascontiguousarray(a) for name, a in arrays.items()}
    nc = _bacc.Bacc("TRN2", target_bir_lowering=False, num_devices=1)
    dram = {name: nc.dram_tensor(name + "_dram", a.shape, _mybir.dt.from_np(a.dtype), kind="ExternalInput").ap()
            for name, a in arrays.items()}
    out = nc.dram_tensor("out_dram", tuple(x.shape), _mybir.dt.from_np(_np.dtype("float32")), kind="ExternalOutput").ap()
    build_program(nc, out=out, **dram)
    r = _run(nc, [{name + "_dram": a for name, a in arrays.items()}], core_ids=[0])
    return r.results[0]["out_dram"]
```
